# Optimizing a Trainium2 kernel written in Bass

```python
import numpy as np
import jax
import jax.numpy as jnp

def _softmax(x, axis=-1):
    return jax.nn.softmax(x, axis=axis)

def _gelu(x):
    return jax.nn.gelu(x, approximate=True)

def _silu(x):
    return jax.nn.silu(x)

def _sigmoid(x):
    return jax.nn.sigmoid(x)

def _layernorm(x, axis=-1, eps=1e-05):
    m = jnp.mean(x, axis=axis, keepdims=True)
    v = jnp.var(x, axis=axis, keepdims=True)
    return (x - m) / jnp.sqrt(v + eps)

def _scatter_add(tgt, idx, src, axis=0):
    return tgt.at[idx].add(src)

def _segment_sum(src, seg, n):
    return jax.ops.segment_sum(src, seg, n)
kernel_name = 'mk_adaln_d1_jaxref_r4_d78bc2'

def setup_inputs(seed: int=0):
    np.random.seed(seed)
    _w = jnp.asarray

    def _L0_attn_setup():
        import jax, jax.numpy as jnp
        import numpy as np
        B, N, D_IN, D_OUT, H = (2, 512, 256, 256, 16)
        HEAD_DIM = D_OUT // H
        key = jax.random.key(seed)
        ks = jax.random.split(key, 8)
        s = 0.02
        return {'x': jax.random.normal(ks[0], (B, N, D_IN), dtype=jnp.float32), 'Wq': jax.random.normal(ks[1], (D_IN, D_OUT), dtype=jnp.float32) * s, 'Wk': jax.random.normal(ks[2], (D_IN, D_OUT), dtype=jnp.float32) * s, 'Wv': jax.random.normal(ks[3], (D_IN, D_OUT), dtype=jnp.float32) * s, 'Wo': jax.random.normal(ks[4], (D_OUT, D_OUT), dtype=jnp.float32) * s, 'bo': jnp.zeros((D_OUT,), dtype=jnp.float32), 'w': jax.random.uniform(ks[5], (H,), dtype=jnp.float32), 'v': jax.random.uniform(ks[6], (H,), dtype=jnp.float32)}
    _L0_attn_in = _L0_attn_setup()

    def _L0_ffn_setup():
        import jax, jax.numpy as jnp
        import numpy as np
        BS, SLEN, DIM = (1, 512, 256)
        NUM_EXPERTS, TOP_K = (8, 2)
        HID = 352

        def _masked_grouped_mm(x, w, onehot):
            g = jnp.einsum('tk,gnk->tgn', x, w, preferred_element_type=jnp.float32)
            return jnp.einsum('tgn,tg->tn', g, onehot)

        def moe_forward(x, gate_w, expert_bias, w_up, w_down, shared_w_up, shared_w_down):
            bs, slen, dim = x.shape
            xf = x.reshape(-1, dim)
            scores = jax.nn.sigmoid((xf @ gate_w.T).astype(jnp.float32))
            biased = scores + expert_bias
            _, sel = jax.lax.top_k(biased, TOP_K)
            top_scores = jnp.take_along_axis(scores, sel, axis=-1)
            flat_sel = sel.reshape(-1)
            counts = jnp.bincount(flat_sel, length=NUM_EXPERTS)
            order = jnp.argsort(flat_sel, stable=True)
            scores_sorted = top_scores.reshape(-1)[order]
            token_ids = order // TOP_K
            routed_in = (xf[token_ids] * scores_sorted[:, None]).astype(x.dtype)
            seg = jnp.repeat(jnp.arange(NUM_EXPERTS), counts, total_repeat_length=flat_sel.shape[0])
            onehot = jax.nn.one_hot(seg, NUM_EXPERTS, dtype=jnp.float32)
            h = _masked_grouped_mm(routed_in.astype(jnp.bfloat16), w_up.astype(jnp.bfloat16), onehot)
            h = jnp.square(jax.nn.relu(h.astype(jnp.bfloat16)))
            routed_out = _masked_grouped_mm(h.astype(jnp.bfloat16), w_down.astype(jnp.bfloat16), onehot)
            routed_out = routed_out.astype(jnp.bfloat16).astype(x.dtype)
            hs = jnp.square(jax.nn.relu(xf @ shared_w_up.T))
            shared_out = hs @ shared_w_down.T
            combined = jnp.zeros((flat_sel.shape[0], dim), routed_out.dtype).at[order].set(routed_out)
            out = combined.reshape(-1, TOP_K, dim).sum(axis=1) + shared_out
            return out.reshape(bs, slen, dim)
        key = jax.random.key(seed)
        k = jax.random.split(key, 6)
        s = 0.02
        return {'x': jax.random.normal(k[0], (BS, SLEN, DIM), jnp.float32), 'gate_w': jax.random.normal(k[1], (NUM_EXPERTS, DIM), jnp.float32) * s, 'expert_bias': jnp.zeros((NUM_EXPERTS,), jnp.float32), 'w_up': jax.random.normal(k[2], (NUM_EXPERTS, HID, DIM), jnp.float32) * s, 'w_down': jax.random.normal(k[3], (NUM_EXPERTS, DIM, HID), jnp.float32) * s, 'shared_w_up': jax.random.normal(k[4], (HID, DIM), jnp.float32) * s, 'shared_w_down': jax.random.normal(k[5], (DIM, HID), jnp.float32) * s}
    _L0_ffn_in = _L0_ffn_setup()
    _L0_c = _w((lambda *s: np.random.randn(*s).astype(np.float32) * 0.05)(16, 256))
    _L0_wmod = _w((lambda *s: np.random.randn(*s).astype(np.float32) * 0.05)(256, 6 * 256) * 256 ** (-0.5))
    _d = {'L0_attn_x': _L0_attn_in['x'], 'L0_attn_Wq': _L0_attn_in['Wq'], 'L0_attn_Wk': _L0_attn_in['Wk'], 'L0_attn_Wv': _L0_attn_in['Wv'], 'L0_attn_Wo': _L0_attn_in['Wo'], 'L0_attn_bo': _L0_attn_in['bo'], 'L0_attn_w': _L0_attn_in['w'], 'L0_attn_v': _L0_attn_in['v'], 'L0_ffn_gate_w': _L0_ffn_in['gate_w'], 'L0_ffn_expert_bias': _L0_ffn_in['expert_bias'], 'L0_ffn_w_up': _L0_ffn_in['w_up'], 'L0_ffn_w_down': _L0_ffn_in['w_down'], 'L0_ffn_shared_w_up': _L0_ffn_in['shared_w_up'], 'L0_ffn_shared_w_down': _L0_ffn_in['shared_w_down'], 'L0_c': _L0_c, 'L0_wmod': _L0_wmod}
    _x0 = _d['L0_attn_x']
    _d['L0_attn_x'] = jax.random.normal(jax.random.fold_in(jax.random.key(seed), 1), (16, 512, 256), dtype=_x0.dtype)
    del _x0
    return _d

def reference(L0_attn_x, L0_attn_Wq, L0_attn_Wk, L0_attn_Wv, L0_attn_Wo, L0_attn_bo, L0_attn_w, L0_attn_v, L0_ffn_gate_w, L0_ffn_expert_bias, L0_ffn_w_up, L0_ffn_w_down, L0_ffn_shared_w_up, L0_ffn_shared_w_down, L0_c, L0_wmod):

    def _L0_attn_ref(x, Wq, Wk, Wv, Wo, bo, w, v):
        import jax, jax.numpy as jnp
        import numpy as np
        B, N, D_IN, D_OUT, H = (2, 512, 256, 256, 16)
        HEAD_DIM = D_OUT // H
        b, n, _ = x.shape
        h = w.shape[0]
        hd = Wq.shape[1] // h

        def proj(W):
            return (x @ W).reshape(b, n, h, hd).transpose(0, 2, 1, 3)
        q, k, val = (proj(Wq), proj(Wk), proj(Wv))
        pos = jnp.arange(n)
        R = jnp.abs(pos[:, None] - pos[None, :]).astype(x.dtype)
        wv = w[:, None, None]
        vv = v[:, None, None]
        R_hat = (1.0 + jnp.exp(vv)) / (1.0 + jnp.exp(vv - wv * R))
        scores = jax.nn.relu(jnp.einsum('bhqd,bhkd->bhqk', q, k)) * R_hat[None]
        causal = jnp.triu(jnp.ones((n, n), dtype=bool), k=1)
        scores = jnp.where(causal[None, None], -jnp.inf, scores)
        attn = jax.nn.softmax(scores / np.sqrt(hd).astype(x.dtype), axis=-1)
        ctx = jnp.einsum('bhqk,bhkd->bhqd', attn, val)
        ctx = ctx.transpose(0, 2, 1, 3).reshape(b, n, h * hd)
        return ctx @ Wo + bo

    def _L0_ffn_ref(x, gate_w, expert_bias, w_up, w_down, shared_w_up, shared_w_down):
        import jax, jax.numpy as jnp
        import numpy as np
        BS, SLEN, DIM = (1, 512, 256)
        NUM_EXPERTS, TOP_K = (8, 2)
        HID = 352

        def _masked_grouped_mm(x, w, onehot):
            g = jnp.einsum('tk,gnk->tgn', x, w, preferred_element_type=jnp.float32)
            return jnp.einsum('tgn,tg->tn', g, onehot)

        def moe_forward(x, gate_w, expert_bias, w_up, w_down, shared_w_up, shared_w_down):
            bs, slen, dim = x.shape
            xf = x.reshape(-1, dim)
            scores = jax.nn.sigmoid((xf @ gate_w.T).astype(jnp.float32))
            biased = scores + expert_bias
            _, sel = jax.lax.top_k(biased, TOP_K)
            top_scores = jnp.take_along_axis(scores, sel, axis=-1)
            flat_sel = sel.reshape(-1)
            counts = jnp.bincount(flat_sel, length=NUM_EXPERTS)
            order = jnp.argsort(flat_sel, stable=True)
            scores_sorted = top_scores.reshape(-1)[order]
            token_ids = order // TOP_K
            routed_in = (xf[token_ids] * scores_sorted[:, None]).astype(x.dtype)
            seg = jnp.repeat(jnp.arange(NUM_EXPERTS), counts, total_repeat_length=flat_sel.shape[0])
            onehot = jax.nn.one_hot(seg, NUM_EXPERTS, dtype=jnp.float32)
            h = _masked_grouped_mm(routed_in.astype(jnp.bfloat16), w_up.astype(jnp.bfloat16), onehot)
            h = jnp.square(jax.nn.relu(h.astype(jnp.bfloat16)))
            routed_out = _masked_grouped_mm(h.astype(jnp.bfloat16), w_down.astype(jnp.bfloat16), onehot)
            routed_out = routed_out.astype(jnp.bfloat16).astype(x.dtype)
            hs = jnp.square(jax.nn.relu(xf @ shared_w_up.T))
            shared_out = hs @ shared_w_down.T
            combined = jnp.zeros((flat_sel.shape[0], dim), routed_out.dtype).at[order].set(routed_out)
            out = combined.reshape(-1, TOP_K, dim).sum(axis=1) + shared_out
            return out.reshape(bs, slen, dim)
        return moe_forward(x, gate_w, expert_bias, w_up, w_down, shared_w_up, shared_w_down)
    x = L0_attn_x
    mod = (_silu(L0_c) @ L0_wmod).reshape(L0_c.shape[0], 6, 1, -1)
    sa, ca, ga, sb, cb, gb = (mod[:, 0], mod[:, 1], mod[:, 2], mod[:, 3], mod[:, 4], mod[:, 5])
    ga = (2 * (ga >= 0) - 1) * jnp.maximum(jnp.abs(ga), 0.25)
    gb = (2 * (gb >= 0) - 1) * jnp.maximum(jnp.abs(gb), 0.25)
    h = _layernorm(x, axis=-1) * (1 + ca) + sa
    x = x + ga * _L0_attn_ref(h, L0_attn_Wq, L0_attn_Wk, L0_attn_Wv, L0_attn_Wo, L0_attn_bo, L0_attn_w, L0_attn_v)
    h = _layernorm(x, axis=-1) * (1 + cb) + sb
    x = x + gb * _L0_ffn_ref(h, L0_ffn_gate_w, L0_ffn_expert_bias, L0_ffn_w_up, L0_ffn_w_down, L0_ffn_shared_w_up, L0_ffn_shared_w_down)
    return x

_drawn_inputs = setup_inputs


def setup_inputs(seed=0):
    import zlib

    import numpy as np

    out = dict(_drawn_inputs(seed))
    spreads = {'L0_attn_bo': (0.0, 0.331), 'L0_ffn_expert_bias': (0.0, 0.8)}
    factors = {'L0_attn_Wq': 8.0,
     'L0_attn_Wk': 8.0,
     'L0_attn_Wv': 8.0,
     'L0_attn_Wo': 8.0,
     'L0_attn_w': 8.0,
     'L0_attn_v': 8.0,
     'L0_ffn_gate_w': 8.0,
     'L0_ffn_w_up': 8.0,
     'L0_ffn_w_down': 8.0,
     'L0_ffn_shared_w_up': 5.242,
     'L0_ffn_shared_w_down': 4.798}
    for name, (base, spread) in spreads.items():
        noise = np.random.default_rng([zlib.crc32(name.encode()), seed]).standard_normal(out[name].shape)
        drawn = base * np.exp(spread * noise) if base else spread * noise
        out[name] = jnp.asarray(drawn.astype(out[name].dtype))
    for name, factor in factors.items():
        out[name] = (out[name] * factor).astype(out[name].dtype)
    return out
```

```python
from contextlib import ExitStack

import concourse.bass as bass
from concourse import mybir
from concourse.alu_op_type import AluOpType as ALU

ACT = mybir.ActivationFunctionType
F32 = mybir.dt.float32
BF16 = mybir.dt.bfloat16
U32 = mybir.dt.uint32
I32 = mybir.dt.int32
AX = mybir.AxisListType

P = 128
B, N, D = 16, 512, 256
H, HD = 16, 16
E, HID = 8, 352
T = N // P
KD = D // P
HP = H // 2
STEPS = HP * B
PARTS = 3
STACK = 96
EPS = 1e-5
SA, CA, GA, SB, CB, GB = range(6)
ROWW = D + 2
BIG = T * P
CAP = B * N + BIG
TILES = 2 * B * N // BIG + E
CHAIN = 12 + 2 * T
RING = 4
AHEAD = 3
HT = [(0, 128), (128, 128), (256, 96)]


def pairs(eng, first, last, step):
    n = (last - first) // 2
    if n:
        with eng.Fori(0, n) as i:
            for u in range(2):
                step(i * 2 + (first + u), (first + u) % 2)
    if (last - first) % 2:
        step(last - 1, (last - 1) % 2)


class Kit:

    def __init__(self, nc, ctx, stage):
        self.nc, self.ctx, self.stage = nc, ctx, stage

    def sb(self, name, shape, dt=F32):
        return self.ctx.enter_context(self.nc.sbuf_tensor(self.stage + name, shape, dt))

    def ps(self, name, shape, dt=F32):
        return self.ctx.enter_context(self.nc.psum_tensor(self.stage + name, shape, dt))

    def sem(self, name):
        return self.ctx.enter_context(self.nc.semaphore(self.stage + name))


def prepare(nc, a, keep, dram):
    with ExitStack() as ctx:
        kit = Kit(nc, ctx, "prep_")
        cT = kit.sb("cT", [P, KD, B])
        wmod = kit.sb("wmod", [P, KD, 6 * D])
        e = kit.sb("e", [P, KD, B])
        e1 = kit.sb("e1", [P, KD, B])
        er = kit.sb("er", [P, KD, B])
        sT = kit.sb("sT", [P, KD, B])
        wrow = kit.sb("wrow", [P, H])
        vrow = kit.sb("vrow", [P, H])
        nw = kit.sb("nw", [P, H])
        ev = kit.sb("ev", [P, H])
        top = kit.sb("top", [P, H])
        dist = kit.sb("dist", [P, N])
        dpos = kit.sb("dpos", [P, N])
        den = kit.sb("den", [P, 2, N])
        den1 = kit.sb("den1", [P, 2, N])
        rec = kit.sb("rec", [P, 2, N])
        tab = kit.sb("tab", [P, 2, N])
        g = kit.sb("g", [B, 2, D])
        gneg = kit.sb("gneg", [B, 2, D])
        gmag = kit.sb("gmag", [B, 2, D])
        gsgn = kit.sb("gsgn", [B, 2, D])
        gsg2 = kit.sb("gsg2", [B, 2, D])
        gate = kit.sb("gate", [B, 2, D])
        ones = kit.sb("ones", [P, P])
        modT_ps = kit.ps("modT_ps", [P, 2, KD, B])
        mod2 = kit.sb("mod2", [B, 2, D])
        mod2_ps = kit.ps("mod2_ps", [B, 2, D])
        gate_ps = kit.ps("gate_ps", [B, 2, D])

        loaded = kit.sem("loaded")
        wv_in = kit.sem("wv_in")
        exp_c = kit.sem("exp_c")
        silu = kit.sem("silu")
        mod_ps = kit.sem("mod_ps")
        gate_done = kit.sem("gate_done")
        dist_done = kit.sem("dist_done")
        dpos_done = kit.sem("dpos_done")
        nw_done = kit.sem("nw_done")
        ev_done = kit.sem("ev_done")
        top_done = kit.sem("top_done")
        den_done = kit.sem("den_done")
        chain = kit.sem("chain")
        tab_raw = kit.sem("tab_raw")
        tab_done = kit.sem("tab_done")
        tab_out = [kit.sem(f"tab_out{s}") for s in range(2)]
        gate_out = kit.sem("gate_out")
        ones_done = kit.sem("ones_done")
        tabs_in = kit.sem("tabs_in")
        MODS = [SA, CA]

        with nc.Block() as block:

            @block.sync
            def _(sp):
                sp.dma_start(cT[:, :, :], a["cT"].rearrange("(k p) b -> p k b", p=P)).then_inc(loaded, 16)
                sp.dma_start(wmod[:, :, :], a["wmod"].rearrange("(k p) n -> p k n", p=P)).then_inc(loaded, 16)
                sp.dma_start(wrow[:, :], a["w"].unsqueeze(0).partition_broadcast(P)).then_inc(wv_in, 16)
                sp.dma_start(vrow[:, :], a["v"].unsqueeze(0).partition_broadcast(P)).then_inc(wv_in, 16)
                for h in range(H):
                    sp.wait_ge(tab_done, h + 1)
                    sp.dma_start(dram["table"][h // 2, :, h % 2, :], tab[:, h % 2, :]).then_inc(tab_out[h % 2], 16)
                sp.wait_ge(gate_done, 3)
                sp.dma_start(dram["rows"][:, 0:2, :], gate[:, :, :]).then_inc(gate_out, 16)
                sp.dma_start(dram["rows"][:, 2:4, :], mod2[:, :, :]).then_inc(gate_out, 16)
                for s in range(2):
                    sp.wait_ge(tab_out[s], 16 * (H // 2))
                sp.wait_ge(gate_out, 32)

            @block.scalar
            def _(act):
                act.wait_ge(loaded, 32)
                nc.scalar.activation(e[:, :, :], cT[:, :, :], ACT.Exp, scale=-1.0).then_inc(exp_c, 1)
                act.wait_ge(wv_in, 32)
                nc.scalar.activation(ev[:, :], vrow[:, :], ACT.Exp).then_inc(ev_done, 1)
                act.wait_ge(nw_done, 1)
                act.wait_ge(dpos_done, 1)
                for h in range(H):
                    if h >= 2:
                        act.wait_ge(chain, h - 1)
                    nc.scalar.activation(den[:, h % 2, :], dpos[:, :], ACT.Exp, bias=vrow[:, h:h + 1],
                                         scale=nw[:, h:h + 1]).then_inc(den_done, 1)

            @block.gpsimd
            def _(pool):
                nc.gpsimd.iota(dist[:, :], pattern=[[-1, N]], base=(T - 1) * P, channel_multiplier=1,
                               allow_small_or_imprecise_dtypes=True).then_inc(dist_done, 1)
                nc.gpsimd.memset(ones[:, :], 1.0).then_inc(ones_done, 1)
                pool.wait_ge(ones_done, 1)
                nc.gpsimd.affine_select(keep["ident"][:, :], ones[:, :], pattern=[[-1, P]], compare_op=ALU.is_equal,
                                        fill=0.0, base=0, channel_multiplier=1)
                for h in range(H):
                    pool.wait_ge(tab_raw, h + 1)
                    if h >= 2:
                        pool.wait_ge(tab_out[h % 2], 16 * (h // 2))
                    nc.gpsimd.affine_select(tab[:, h % 2, :], rec[:, h % 2, :], pattern=[[-1, N]],
                                            compare_op=ALU.is_ge, fill=0.0, base=(T - 1) * P,
                                            channel_multiplier=1).then_inc(tab_done, 1)

            @block.tensor
            def _(pe):
                pe.wait_ge(silu, 1)
                for c, chunk in enumerate(MODS):
                    for j in range(KD):
                        for k in range(KD):
                            col = chunk * D + j * P
                            nc.tensor.matmul(modT_ps[:, c, j, :], wmod[:, k, col:col + P], sT[:, k, :],
                                             start=(k == 0), stop=(k == KD - 1))
                for c, chunk in enumerate([GA, GB, CB, SB]):
                    rows_ps = gate_ps if c < 2 else mod2_ps
                    for k in range(KD):
                        last = nc.tensor.matmul(rows_ps[:, c % 2, :], sT[:, k, :], wmod[:, k, chunk * D:(chunk + 1) * D],
                                                start=(k == 0), stop=(k == KD - 1))
                last.then_inc(mod_ps, 1)

            @block.vector
            def _(dve):
                step = [0]

                def after(ins, sem):
                    step[0] += 1
                    ins.then_inc(sem, 1)
                    dve.wait_ge(sem, step[0])

                own = kit.sem("own")
                dve.wait_ge(exp_c, 1)
                after(nc.vector.tensor_scalar(e1[:, :, :], e[:, :, :], 1.0, None, ALU.add), own)
                after(nc.vector.reciprocal(er[:, :, :], e1[:, :, :]), own)
                nc.vector.tensor_tensor(sT[:, :, :], cT[:, :, :], er[:, :, :], ALU.mult).then_inc(silu, 1)
                dve.wait_ge(wv_in, 32)
                nc.vector.tensor_scalar(nw[:, :], wrow[:, :], -1.0, None, ALU.mult).then_inc(nw_done, 1)
                dve.wait_ge(dist_done, 1)
                nc.vector.tensor_scalar(dpos[:, :], dist[:, :], 0.0, None, ALU.max).then_inc(dpos_done, 1)
                dve.wait_ge(ev_done, 1)
                after(nc.vector.tensor_scalar(top[:, :], ev[:, :], 1.0, HD ** -0.5, ALU.add, ALU.mult), own)
                dve.wait_ge(mod_ps, 1)
                for c in range(2):
                    nc.vector.tensor_scalar(mod2[:, c, :], mod2_ps[:, c, :], 1.0 - c, None, ALU.add
                                            ).then_inc(gate_done, 1)
                for c in range(2):
                    nc.vector.tensor_scalar(keep["modT"][:, c, :, :], modT_ps[:, c, :, :], float(c % 2), None, ALU.add)
                after(nc.vector.tensor_copy(g[:, :, :], gate_ps[:, :, :]), own)
                after(nc.vector.tensor_scalar(gneg[:, :, :], g[:, :, :], -1.0, 0.25, ALU.mult, ALU.max), own)
                after(nc.vector.tensor_tensor(gmag[:, :, :], g[:, :, :], gneg[:, :, :], ALU.max), own)
                after(nc.vector.tensor_scalar(gsgn[:, :, :], g[:, :, :], 0.0, 2.0, ALU.is_ge, ALU.mult), own)
                after(nc.vector.tensor_scalar(gsg2[:, :, :], gsgn[:, :, :], 1.0, None, ALU.subtract), own)
                nc.vector.tensor_tensor(gate[:, :, :], gmag[:, :, :], gsg2[:, :, :], ALU.mult).then_inc(gate_done, 1)
                for h in range(H):
                    s = h % 2
                    dve.wait_ge(den_done, h + 1)
                    nc.vector.tensor_scalar(den1[:, s, :], den[:, s, :], 1.0, None, ALU.add).then_inc(chain, 1)
                    dve.wait_ge(chain, h + 1)
                    after(nc.vector.reciprocal(den1[:, s, :], den1[:, s, :]), own)
                    if h >= 2:
                        dve.wait_ge(tab_done, h - 1)
                    nc.vector.tensor_scalar(rec[:, s, :], den1[:, s, :], top[:, h:h + 1], None,
                                            ALU.mult).then_inc(tab_raw, 1)


def project(nc, a, keep, dram, V_all):
    with ExitStack() as ctx:
        kit = Kit(nc, ctx, "proj_")
        ident, modT = keep["ident"], keep["modT"]
        w = {n: kit.sb(n, [P, KD, D]) for n in ("Wq", "Wk", "Wv")}
        x = kit.sb("x", [P, 2, T, D])
        stats = kit.sb("stats", [P, 2, T, 6])
        mv = kit.sb("mv", [P, 2, T, 2])
        var = kit.sb("var", [P, 2, T])
        rstd = kit.sb("rstd", [P, 2, T])
        xn = kit.sb("xn", [P, 2, T, D])
        hT = kit.sb("hT", [P, 2, KD, N])
        rest = kit.sb("rest", [P, 2 * KD, N])
        part = kit.sb("part", [P, 2, 2 * KD, PARTS, N], BF16)
        half = kit.sb("half", [P, T])
        tp = [kit.ps(f"tp{j}", [P, N]) for j in range(KD)]
        qk = [kit.ps(f"qk{m}", [P, N]) for m in range(2 * KD)]
        vp = [kit.ps(f"vp{m}", [P, 2, D]) for m in range(2)]

        w_in = kit.sem("w_in")
        x_in = [kit.sem(f"x_in{s}") for s in range(2)]
        half_set = kit.sem("half_set")
        stats_done = kit.sem("stats_done")
        mv_done = kit.sem("mv_done")
        held = kit.sem("held")
        var_done = kit.sem("var_done")
        rstd_done = kit.sem("rstd_done")
        xn_done = kit.sem("xn_done")
        tp_done = kit.sem("tp_done")
        hT_done = kit.sem("hT_done")
        qk_done = kit.sem("qk_done")
        vp_done = kit.sem("vp_done")
        v_out = kit.sem("v_out")
        part1 = kit.sem("part1")
        rest_done = kit.sem("rest_done")
        part2 = kit.sem("part2")
        part3 = kit.sem("part3")
        stored = [kit.sem(f"stored{s}") for s in range(2)]
        M = 2 * KD
        slot1 = [2, 2, 0, 0]
        slot3 = [0, 0, 2, 2]

        with nc.Block() as block:

            @block.sync
            def _(sp):
                for n in w:
                    sp.dma_start(w[n][:, :, :], a[n].rearrange("(k p) n -> p k n", p=P)).then_inc(w_in, 16)

                def load(b, s):
                    if not isinstance(b, int) or b >= 2:
                        sp.wait_ge(xn_done, b * T - T)
                    sp.dma_start(x[:, s, :, :], a["x"][b].rearrange("(t p) d -> p t d", p=P)).then_inc(x_in[s], 16)

                def store(b, s):
                    for m in range(M):
                        sp.wait_ge(part3, b * M + (m + 1))
                        dst = dram["q" if m < KD else "k"]
                        g = HP // KD
                        for r in range(PARTS):
                            sp.dma_start(dst[(m % KD) * g:(m % KD + 1) * g, b, r],
                                         part[:, s, m, r, :]).then_inc(stored[s], 16)

                load(0, 0)
                def step(b, s):
                    load(b, s)
                    store(b - 1, 1 - s)
                step(1, 1)
                pairs(sp, 2, B, step)
                store(B - 1, (B - 1) % 2)
                for s in range(2):
                    sp.wait_ge(stored[s], 16 * (B // 2) * M * PARTS)

            @block.gpsimd
            def _(pool):
                nc.gpsimd.memset(half[:, :], -0.5).then_inc(half_set, 1)
                pool.wait_ge(half_set, 1)

                def root(b, s):
                    pool.wait_ge(var_done, b + 1)
                    nc.gpsimd.tensor_tensor(rstd[:, s, :], var[:, s, :], half[:, :], ALU.pow).then_inc(rstd_done, 1)

                def step(b, s, ahead=True):
                    if ahead:
                        root(b + 1, 1 - s)
                    for m in range(M):
                        pool.wait_ge(part2, b * M + (m + 1))
                        nc.gpsimd.tensor_tensor(part[:, s, m, slot3[m], :], rest[:, m, :], part[:, s, m, 1, :],
                                                ALU.subtract).then_inc(part3, 1)

                root(0, 0)
                step(0, 0)
                pairs(pool, 1, B - 1, step)
                step(B - 1, (B - 1) % 2, ahead=False)

            @block.vector
            def _(dve):
                def norm(b, s):
                    dve.wait_ge(x_in[s], (b // 2 + 1) * 16)
                    for t in range(T):
                        nc.vector.bn_stats(stats[:, s, t, :], x[:, s, t, :]).then_inc(stats_done, 1)
                    dve.wait_ge(stats_done, b * T + T)
                    dve.sem_inc(held, 1)
                    for t in range(T):
                        nc.vector.bn_aggr(mv[:, s, t, :], stats[:, s, t, :]).then_inc(mv_done, 1)
                    dve.wait_ge(mv_done, b * T + T)
                    nc.vector.tensor_scalar(var[:, s, :], mv[:, s, :, 1], EPS, None, ALU.add).then_inc(var_done, 1)

                def scale(b, s):
                    dve.wait_ge(rstd_done, b + 1)
                    for t in range(T):
                        last = nc.vector.tensor_scalar(xn[:, s, t, :], x[:, s, t, :], mv[:, s, t, 0:1],
                                                       rstd[:, s, t:t + 1], ALU.subtract, ALU.mult)
                        last.then_inc(xn_done, 1)

                def split(b, s, m):
                    dve.wait_ge(part1, b * M + (m + 1))
                    if not isinstance(b, int) or b:
                        dve.wait_ge(part3, (b - 1) * M + (m + 1))
                    nc.vector.tensor_tensor(rest[:, m, :], qk[m][:, :], part[:, s, m, slot1[m], :],
                                            ALU.subtract).then_inc(rest_done, 1)

                def round2(b, s, m):
                    dve.wait_ge(rest_done, b * M + (m + 1))
                    nc.vector.tensor_copy(part[:, s, m, 1, :], rest[:, m, :]).then_inc(part2, 1)

                def step(b, s, ahead=True):
                    if ahead:
                        norm(b + 1, 1 - s)
                    split(b, s, 0)
                    split(b, s, 1)
                    if ahead:
                        scale(b + 1, 1 - s)
                    round2(b, s, 0)
                    split(b, s, 2)
                    round2(b, s, 1)
                    split(b, s, 3)
                    round2(b, s, 2)
                    round2(b, s, 3)

                norm(0, 0)
                scale(0, 0)
                step(0, 0)
                pairs(dve, 1, B - 1, step)
                step(B - 1, (B - 1) % 2, ahead=False)

            @block.tensor
            def _(pe):
                def turn(b, s):
                    pe.wait_ge(xn_done, b * T + T)
                    for j in range(KD):
                        if not isinstance(b, int) or b:
                            pe.wait_ge(hT_done, (b - 1) * KD + (j + 1))
                        for t in range(T):
                            last = nc.tensor.transpose(tp[j][:, t * P:(t + 1) * P], xn[:, s, t, j * P:(j + 1) * P],
                                                       ident[:, :])
                        last.then_inc(tp_done, 1)

                def project_qk(b, s):
                    pe.wait_ge(hT_done, b * KD + KD)
                    for m in range(M):
                        if not isinstance(b, int) or b:
                            pe.wait_ge(rest_done, (b - 1) * M + (m + 1))
                        src = w["Wq"] if m < KD else w["Wk"]
                        for k in range(KD):
                            last = nc.tensor.matmul(qk[m][:, :], src[:, k, (m % KD) * P:(m % KD + 1) * P],
                                                    hT[:, s, k, :], start=(k == 0), stop=(k == KD - 1))
                        last.then_inc(qk_done, 1)

                def project_v(b, s):
                    for m in range(2):
                        if not isinstance(b, int) or b:
                            pe.wait_ge(v_out, (b - 1) * 2 + (m + 1))
                        for t2 in range(2):
                            t = 2 * m + t2
                            for k in range(KD):
                                last = nc.tensor.matmul(vp[m][:, t2, :], hT[:, s, k, t * P:(t + 1) * P],
                                                        w["Wv"][:, k, :], start=(k == 0), stop=(k == KD - 1))
                        last.then_inc(vp_done, 1)

                def step(b, s, ahead=True):
                    project_qk(b, s)
                    if ahead:
                        turn(b + 1, 1 - s)
                    project_v(b, s)

                pe.wait_ge(w_in, 48)
                turn(0, 0)
                step(0, 0)
                pairs(pe, 1, B - 1, step)
                step(B - 1, (B - 1) % 2, ahead=False)

            @block.scalar
            def _(act):
                def modulate(b, s):
                    for j in range(KD):
                        act.wait_ge(tp_done, b * KD + (j + 1))
                        if not isinstance(b, int) or b >= 2:
                            act.wait_ge(vp_done, (b - 2) * 2 + 2)
                        nc.scalar.activation(hT[:, s, j, :], tp[j][:, :], ACT.Identity,
                                             bias=modT[:, 0, j, bass.ds(b, 1)],
                                             scale=modT[:, 1, j, bass.ds(b, 1)]).then_inc(hT_done, 1)

                def first(b, s, m):
                    act.wait_ge(qk_done, b * M + (m + 1))
                    if not isinstance(b, int) or b >= 2:
                        act.wait_ge(stored[s], (b // 2) * (16 * M * PARTS))
                    nc.scalar.copy(part[:, s, m, slot1[m], :], qk[m][:, :]).then_inc(part1, 1)

                def values(b, m):
                    act.wait_ge(vp_done, b * 2 + (m + 1))
                    for t2 in range(2):
                        last = nc.scalar.copy(
                            V_all[:, :, :].rearrange("p (g b) c -> p g b c", b=B)
                            [:, :, b, (2 * m + t2) * 32:(2 * m + t2) * 32 + 32],
                            vp[m][:, t2, :].rearrange("p (g c) -> p g c", c=32))
                    last.then_inc(v_out, 1)

                def step(b, s, ahead=True):
                    for m in range(M):
                        first(b, s, m)
                    if ahead:
                        modulate(b + 1, 1 - s)
                    for m in range(2):
                        values(b, m)

                modulate(0, 0)
                step(0, 0)
                step(1, 1)
                pairs(act, 2, B - 1, step)
                step(B - 1, (B - 1) % 2, ahead=False)


def attend(nc, a, keep, dram, V_all):
    units = [[(0, 3, 0)], [(0, 0, 0), (0, 2, P)], [(1, 3, 0)], [(1, 0, 0), (1, 2, P)], [(0, 1, 0), (1, 1, 2 * P)]]
    NU = len(units)
    NX = sum(len(u) for u in units)
    ROW = N + P
    with ExitStack() as ctx:
        kit = Kit(nc, ctx, "att_")
        ident = keep["ident"]
        Q = kit.sb("Q", [STACK, 2, 2 * N], BF16)
        K = kit.sb("K", [STACK, 2, 2 * N], BF16)
        table = kit.sb("table", [P, 2, N])
        V = kit.sb("V", [P, 2, T, 2, 2 * HD])
        scaled = kit.sb("scaled", [P, NU, N])
        top = kit.sb("top", [P, NU, 2])
        shifted = kit.sb("shifted", [P, NU, N])
        prob = kit.sb("prob", [P, 2, 2, T * ROW])
        ctxT = kit.sb("ctxT", [4 * HD, 2, N])
        s_ps = [kit.ps(f"s{i}", [P, N]) for i in range(2)]
        t_ps = [kit.ps(f"t{i}", [P, N]) for i in range(2)]
        o_ps = [kit.ps(f"o{i}", [4 * HD, N]) for i in range(2)]

        q_in = [kit.sem(f"q_in{s}") for s in range(2)]
        k_in = [kit.sem(f"k_in{s}") for s in range(2)]
        table_in = kit.sem("table_in")
        ones_set = kit.sem("ones_set")
        v_ready = kit.sem("v_ready")
        scores = kit.sem("scores")
        maxed = kit.sem("maxed")
        relued = kit.sem("relued")
        turned = kit.sem("turned")
        exped = kit.sem("exped")
        masked = kit.sem("masked")
        summed = kit.sem("summed")
        copied = kit.sem("copied")
        stored = [kit.sem(f"stored{s}") for s in range(2)]
        held = kit.sem("held")

        def hold(eng, sem, value):
            eng.wait_ge(sem, value)
            eng.sem_inc(held, 1)

        def bank(banks, s, u):
            return banks[(s + u) % 2]

        with nc.Block() as block:

            @block.sync
            def _(sp):
                def load(n, s):
                    if not isinstance(n, int) or n >= 2:
                        sp.wait_ge(scores, (n - 1) * NU)
                    hp, b = n // B, n % B
                    for name, buf, sem, mid, low in (("q", Q, q_in, 1, 2), ("k", K, k_in, 0, 0)):
                        src = dram[name]
                        sp.dma_start(buf[0:48, s, :], src[hp, b].rearrange("r (d h) n -> (r d) (h n)", h=2)
                                     ).then_inc(sem[s], 16)
                        sp.dma_start(buf[48:80, s, :], src[hp, b, mid:mid + 2].rearrange(
                            "r (d h) n -> (r d) (h n)", h=2)).then_inc(sem[s], 16)
                        sp.dma_start(buf[80:96, s, :], src[hp, b, low].rearrange("(d h) n -> d (h n)", h=2)
                                     ).then_inc(sem[s], 16)

                def load_table(hp):
                    if not isinstance(hp, int) or hp:
                        sp.wait_ge(maxed, hp * (B * NU))
                    sp.dma_start(table[:, :, :], dram["table"][hp]).then_inc(table_in, 16)

                load_table(0)
                load(0, 0)
                load(1, 1)
                pairs(sp, 2, B, load)
                with sp.Fori(1, HP) as hp:
                    load(hp * B, 0)
                    load(hp * B + 1, 1)
                    load_table(hp)
                    with sp.Fori(1, B // 2) as i:
                        load(hp * B + i * 2, 0)
                        load(hp * B + i * 2 + 1, 1)
                for s in range(2):
                    sp.wait_ge(stored[s], 16 * (STEPS // 2))

            @block.gpsimd
            def _(pool):
                nc.gpsimd.memset(V[:, :, :, :, HD:2 * HD], 1.0).then_inc(ones_set, 1)

                def values(n, s):
                    if not isinstance(n, int) or n >= 2:
                        hold(pool, summed, n - 1)
                    nc.gpsimd.tensor_copy(V[:, s, :, :, 0:HD],
                                          V_all[:, n, :].rearrange("p (t h d) -> p t h d", t=T, h=2)
                                          ).then_inc(v_ready, 1)

                def mask(n, s, h):
                    hold(pool, exped, n * NX + (NX - 1 + h))
                    blocks = prob[:, s, h, :].rearrange("p (t n) -> p t n", n=ROW)[:, :, 0:P]
                    nc.gpsimd.affine_select(blocks, blocks, pattern=[[0, T], [1, P]], compare_op=ALU.is_ge,
                                            fill=0.0, base=0, channel_multiplier=-1).then_inc(masked, 1)

                def step(n, s, ahead=True):
                    mask(n, s, 0)
                    mask(n, s, 1)
                    if ahead:
                        values(n + 1, 1 - s)

                values(0, 0)
                step(0, 0)
                pairs(pool, 1, STEPS - 1, step)
                step(STEPS - 1, (STEPS - 1) % 2, ahead=False)

            @block.vector
            def _(dve):
                def maximum(n, s, u):
                    if u == 0:
                        hold(dve, table_in, (n // B + 1) * 16)
                    hold(dve, scores, n * NU + (u + 1))
                    for i, (h, t, c) in enumerate(units[u]):
                        w = (t + 1) * P
                        last = nc.vector.tensor_tensor_reduce(
                            scaled[:, u, c:c + w], bank(s_ps, s, u)[:, c:c + w], table[:, h, N - w:N], 1.0, 0.0,
                            ALU.mult, ALU.max, top[:, u, i:i + 1])
                    last.then_inc(maxed, 1)

                def shift(n, s, u):
                    dve.wait_ge(maxed, n * NU + (u + 1))
                    if not isinstance(n, int) or n:
                        dve.wait_ge(turned, (n - 1) * NU + (u + 1))
                    for i, (h, t, c) in enumerate(units[u]):
                        w = (t + 1) * P
                        last = nc.vector.tensor_scalar(shifted[:, u, c:c + w], scaled[:, u, c:c + w], 0.0,
                                                       top[:, u, i:i + 1], ALU.max, ALU.subtract)
                    last.then_inc(relued, 1)

                def step(n, s, prev=True):
                    for u in range(NU):
                        maximum(n, s, u)
                        if u:
                            shift(n, s, u - 1)
                        elif prev:
                            shift(n - 1, 1 - s, NU - 1)

                step(0, 0, prev=False)
                pairs(dve, 1, STEPS, step)
                shift(STEPS - 1, 1, NU - 1)

            @block.tensor
            def _(pe):
                def score(n, s, u):
                    if u == 0:
                        pe.wait_ge(q_in[s], (n // 2 + 1) * 48)
                        pe.wait_ge(k_in[s], (n // 2 + 1) * 48)
                    if not isinstance(n, int) or n * NU + u >= 2:
                        pe.wait_ge(maxed, n * NU + (u - 1))
                    for h, t, c in units[u]:
                        w = (t + 1) * P
                        last = nc.tensor.matmul(bank(s_ps, s, u)[:, c:c + w], Q[:, s, h * N + t * P:h * N + w],
                                                K[:, s, h * N:h * N + w], start=True, stop=True)
                    last.then_inc(scores, 1)

                def turn(n, s, u):
                    pe.wait_ge(relued, n * NU + (u + 1))
                    if not isinstance(n, int) or n * NU + u >= 2:
                        pe.wait_ge(exped, n * NX + sum(len(x) for x in units[:u - 1]) if u else
                                   (n - 1) * NX + sum(len(x) for x in units[:NU - 1]))
                    for c in range(0, N, P):
                        last = nc.tensor.transpose(bank(t_ps, s, u)[:, c:c + P], shifted[:, u, c:c + P], ident[:, :])
                    last.then_inc(turned, 1)

                def context_of(n, s, j):
                    if j == 0:
                        pe.wait_ge(v_ready, n + 1)
                        if not isinstance(n, int) or n >= 2:
                            pe.wait_ge(copied, n - 1)
                        pe.wait_ge(masked, n * 2 + 2)
                    for h in range(2):
                        rows = prob[:, s, h, 0:T * N].rearrange("p (t n) -> p t n", n=N)[:, j:T, j * P:(j + 1) * P]
                        last = nc.tensor.matmul(
                            o_ps[s][2 * HD * h:2 * HD * (h + 1), j * P:N].rearrange("p (t n) -> p t n", n=P),
                            V[:, s, j, h, :], rows,
                            start=(j == 0), stop=(j == T - 1))
                    if j == T - 1:
                        last.then_inc(summed, 1)

                def step(n, s, prev=True, following=True):
                    for u in range(NU):
                        if u + 2 < NU:
                            score(n, s, u + 2)
                        elif following:
                            score(n + 1, 1 - s, u + 2 - NU)
                        turn(n, s, u)
                        if prev and 1 <= u:
                            context_of(n - 1, 1 - s, u - 1)

                pe.wait_ge(ones_set, 1)
                score(0, 0, 0)
                score(0, 0, 1)
                step(0, 0, prev=False)
                step(1, 1)
                pairs(pe, 2, STEPS - 1, step)
                step(STEPS - 1, 1, following=False)
                for j in range(T):
                    context_of(STEPS - 1, 1, j)

            @block.scalar
            def _(act):
                def copy(n, s):
                    act.wait_ge(summed, n + 1)
                    if not isinstance(n, int) or n >= 2:
                        act.wait_ge(stored[s], (n // 2) * 16)
                    nc.scalar.copy(ctxT[:, s, :], o_ps[s][:, :]).then_inc(copied, 1)

                def store(n, s):
                    act.wait_ge(copied, n + 1)
                    act.dma_start(dram["ctx"][n % B, n // B], ctxT[:, s, :]).then_inc(stored[s], 16)

                def step(n, s, prev=True, before=True):
                    for u in range(NU):
                        act.wait_ge(turned, n * NU + (u + 1))
                        if u == 0 and (not isinstance(n, int) or n >= 2):
                            act.wait_ge(summed, n - 1)
                        for h, t, c in units[u]:
                            w = (t + 1) * P
                            nc.scalar.activation(prob[:, s, h, t * N:t * N + w], bank(t_ps, s, u)[:, c:c + w],
                                                 ACT.Exp).then_inc(exped, 1)
                        if u == 1 and before:
                            store(n - 2, s)
                    if prev:
                        copy(n - 1, 1 - s)

                step(0, 0, prev=False, before=False)
                step(1, 1, before=False)
                pairs(act, 2, STEPS, step)
                copy(STEPS - 1, 1)
                store(STEPS - 2, 0)
                store(STEPS - 1, 1)


def feed(nc, a, keep, dram, X_all, weights):
    up, down = weights
    with ExitStack() as ctx:
        kit = Kit(nc, ctx, "feed_")
        ident = keep["ident"]
        Wo = kit.sb("Wo", [P, KD, D])
        supT = kit.sb("supT", [P, KD, HID])
        sdownT = kit.sb("sdownT", [P, len(HT), D])
        gateT = kit.sb("gateT", [P, KD, E])
        bo = kit.sb("bo", [P, D])
        ebias = kit.sb("ebias", [P, E])
        den = kit.sb("den", [P, B, N // 8])
        half = kit.sb("half", [P, T])
        iota_e = kit.sb("iota_e", [P, E])
        before = kit.sb("before", [P, P], BF16)
        ones = kit.sb("ones", [P, P], BF16)
        x = kit.sb("x", [P, 2, T, D])
        ga = kit.sb("ga", [P, 2, D])
        num = kit.sb("num", [P, 2, KD, N])
        inv = kit.sb("inv", [P, 2, KD, N])
        mod2 = kit.sb("mod2", [P, 2, 2, D])
        gb = kit.sb("gb", [P, 2, D])
        CT = kit.sb("CT", [P, 2, KD, N])
        gabo = kit.sb("gabo", [P, 2, D])
        xb = kit.sb("xb", [P, 2, T, D])
        Wog = kit.sb("Wog", [P, 2, KD, D])
        stats = kit.sb("stats", [P, 2, T, 6])
        mv = kit.sb("mv", [P, 2, T, 2])
        var = kit.sb("var", [P, 2, T])
        rstd = kit.sb("rstd", [P, 2, T])
        xn = kit.sb("xn", [P, T, D])
        xm = kit.sb("xm", [P, T, D])
        h = kit.sb("h", [P, 2, T, D])
        hT = kit.sb("hT", [P, 2, KD, N])
        relu = kit.sb("relu", [P, len(HT), N])
        hid = kit.sb("hid", [P, len(HT), N])
        shared = kit.sb("shared", [P, T, D])
        e = kit.sb("e", [P, T, E])
        e1 = kit.sb("e1", [P, T, E])
        score = kit.sb("score", [P, T, E])
        biased = kit.sb("biased", [P, T, E])
        best = kit.sb("best", [P, T, 8])
        which = kit.sb("which", [P, T, 8], U32)
        whichf = kit.sb("whichf", [P, 2, T])
        hot = kit.sb("hot", [P, 2, T, E])
        picked = kit.sb("picked", [P, T, E], BF16)
        prod = kit.sb("prod", [P, 2, T, E])
        prod2 = kit.sb("prod2", [P, 2, T, E])
        weight = kit.sb("weight", [P, 2, 2, T])
        base = kit.sb("base", [P, 2, E])
        pos = kit.sb("pos", [P, T, E])
        posf = kit.sb("posf", [P, 2, T])
        place = kit.sb("place", [P, 2, 2, T], U32)
        ids = kit.sb("ids", [P, 2, 2, T])
        rows = kit.sb("rows", [P, 2, 2, T, ROWW], BF16)
        ao = [kit.ps(f"ao{i}", [P, 2, D]) for i in range(2)]
        tp = [kit.ps(f"tp{i}", [P, N]) for i in range(KD)]
        hp = [kit.ps(f"hp{i}", [P, N]) for i in range(2)]
        lg = kit.ps("lg", [P, T, E])
        rk = kit.ps("rk", [P, T + 1, E])

        S = {n: kit.sem(n) for n in (
            "w_in", "den_in", "den_done", "inv_out", "set_up", "xb_done", "wog_done", "gabo_done", "ct", "ao_done", "x1",
            "stats", "mv", "var", "rstd", "xn", "xm", "h", "tp", "hT", "logits", "exp", "own", "mask", "rank",
            "place", "weight", "hidden", "relu", "hid", "down", "shared", "x1s", "rows", "ids", "held", "consts",
            "wgt_in", "wgt_zero", "pad_done")}
        ld1 = [kit.sem(f"ld1{s}") for s in range(2)]
        ld2 = [kit.sem(f"ld2{s}") for s in range(2)]
        ld3 = [kit.sem(f"ld3{s}") for s in range(2)]
        sent = [kit.sem(f"sent{s}") for s in range(2)]
        M = len(HT)
        region = dram["region"]

        def later(b, k):
            return not isinstance(b, int) or b >= k

        def hold(eng, sem, value):
            eng.wait_ge(sem, value)
            eng.sem_inc(S["held"], 1)

        def steps(eng, step):
            step(0, 0, False, True, True)
            step(1, 1, True, True, True)
            pairs(eng, 2, B - 2, lambda b, s: step(b, s, True, True, True))
            step(B - 2, 0, True, True, False)
            step(B - 1, 1, True, False, False)

        with nc.Block() as block:

            @block.sync
            def _(sp):
                for dst, src in ((Wo, "Wo"), (supT, "supT"), (gateT, "gateT")):
                    sp.dma_start(dst[:, :, :], a[src].rearrange("(k p) n -> p k n", p=P)).then_inc(S["w_in"], 16)
                for m, (c, size) in enumerate(HT):
                    sp.dma_start(sdownT[0:size, m, :], a["sdownT"][c:c + size]).then_inc(S["w_in"], 16)
                sp.dma_start(bo[:, :], a["bo"].unsqueeze(0).partition_broadcast(P)).then_inc(S["w_in"], 16)
                sp.dma_start(ebias[:, :], a["bias"].unsqueeze(0).partition_broadcast(P)).then_inc(S["w_in"], 16)
                heads = dram["ctx"].rearrange("b g (h r) n -> b (g h) r n", h=2)
                for b in range(B):
                    sp.dma_start(den[:, b, :], heads[b, :, HD, :].rearrange("h (c n) -> h c n", c=8)
                                 ).then_inc(S["den_in"], 16)
                sp.wait_ge(S["den_done"], 1)
                sp.dma_start(dram["inv"].rearrange("b (p n) -> p b n", p=P), den[:, :, :]
                             ).then_inc(S["inv_out"], 16)
                sp.wait_ge(S["inv_out"], 16)
                inv_rows = dram["inv"].rearrange("b (h n) -> b h n", n=N)

                def load(b, s):
                    if later(b, 2):
                        sp.wait_ge(S["xb_done"], b - 1)
                        sp.wait_ge(S["wog_done"], b - 1)
                        sp.wait_ge(S["ct"], b - 1)
                    sp.dma_start(x[:, s, :, :], a["x"][b].rearrange("(t p) d -> p t d", p=P)).then_inc(ld1[s], 16)
                    sp.dma_start(ga[:, s, :], dram["rows"][b, 0:1, :].partition_broadcast(P)).then_inc(ld1[s], 16)
                    for k in range(KD):
                        sp.dma_start(num[:, s, k, :], heads[b, k * 8:(k + 1) * 8, 0:HD, :]).then_inc(ld1[s], 16)
                        sp.dma_start(inv[:, s, k, :], inv_rows[b, k * 8:(k + 1) * 8, :].unsqueeze(1).to_broadcast(
                            [8, HD, N])).then_inc(ld1[s], 16)
                    if later(b, 2):
                        sp.wait_ge(S["h"], b - 1)
                    sp.dma_start(mod2[:, s, :, :], dram["rows"][b, 2:4, :].partition_broadcast(P)).then_inc(ld2[s], 16)
                    if later(b, 2):
                        sp.wait_ge(S["x1s"], b - 1)
                    sp.dma_start(gb[:, s, :], dram["rows"][b, 1:2, :].partition_broadcast(P)).then_inc(ld3[s], 16)

                load(0, 0)
                load(1, 1)
                pairs(sp, 2, B, load)

            @block.gpsimd
            def _(pool):
                nc.gpsimd.memset(half[:, :], -0.5).then_inc(S["set_up"], 1)
                nc.gpsimd.iota(iota_e[:, :], pattern=[[1, E]], base=0, channel_multiplier=0,
                               allow_small_or_imprecise_dtypes=True).then_inc(S["set_up"], 1)
                nc.gpsimd.iota(ids[:, 0, :, :], pattern=[[B * N, 2], [P, T]], base=0, channel_multiplier=1,
                               allow_small_or_imprecise_dtypes=True).then_inc(S["set_up"], 1)
                nc.gpsimd.iota(base[:, 0, :], pattern=[[CAP, E]], base=0, channel_multiplier=0,
                               allow_small_or_imprecise_dtypes=True).then_inc(S["set_up"], 1)
                nc.gpsimd.memset(ones[:, :], 1.0).then_inc(S["set_up"], 1)
                pool.wait_ge(S["set_up"], 5)
                nc.gpsimd.affine_select(before[:, :], ones[:, :], pattern=[[1, P]], compare_op=ALU.is_gt, fill=0.0,
                                        base=0, channel_multiplier=-1).then_inc(S["consts"], 1)
                nc.gpsimd.memset(up[:, :, :, HID:], 0.0).then_inc(S["wgt_zero"], 1)
                pool.wait_ge(S["wgt_zero"], 1)
                nc.gpsimd.memset(down[HID % P:, M - 1, :, :], 0.0).then_inc(S["wgt_zero"], 1)
                pool.wait_ge(S["wgt_zero"], 2)
                for k in range(KD):
                    pool.dma_start(up[:, k, :, 0:HID], a["upT"][k * P:(k + 1) * P]).then_inc(S["wgt_in"], 16)
                for m, (c, size) in enumerate(HT):
                    pool.dma_start(down[0:size, m, :, :], a["downT"][c:c + size]).then_inc(S["wgt_in"], 16)
                pool.wait_ge(S["w_in"], 128)

                def prep(b, s):
                    pool.wait_ge(ld1[s], (b // 2 + 1) * 96)
                    if later(b, 2):
                        pool.wait_ge(S["xb_done"], b - 1)
                    nc.gpsimd.tensor_tensor(gabo[:, s, :], ga[:, s, :], bo[:, :], ALU.mult).then_inc(S["gabo_done"], 1)
                    if later(b, 2):
                        pool.wait_ge(S["x1"], (b - 1) * 2)
                    nc.gpsimd.tensor_tensor(Wog[:, s, :, :], Wo[:, :, :],
                                            ga[:, s, :].unsqueeze(1).to_broadcast([P, KD, D]), ALU.mult
                                            ).then_inc(S["wog_done"], 1)
                    pool.wait_ge(S["gabo_done"], b + 1)
                    nc.gpsimd.tensor_tensor(xb[:, s, :, :], x[:, s, :, :],
                                            gabo[:, s, :].unsqueeze(1).to_broadcast([P, T, D]), ALU.add
                                            ).then_inc(S["xb_done"], 1)

                def root(b, s):
                    pool.wait_ge(S["var"], b + 1)
                    nc.gpsimd.tensor_tensor(rstd[:, s, :], var[:, s, :], half[:, :], ALU.pow).then_inc(S["rstd"], 1)

                def send(b, s):
                    hold(pool, S["place"], b + 1)
                    hold(pool, S["ids"], b + 1)
                    for c in range(2):
                        for t in range(T):
                            hold(pool, S["rows"], b * (2 * T) + (c * T + t + 1))
                            pool.indirect_dma_start(
                                out=region, out_offset=bass.IndirectOffsetOnAxis(ap=place[:, s, c, t:t + 1], axis=0),
                                in_=rows[:, s, c, t, :], in_offset=None).then_inc(sent[s], 16)

                prep(0, 0)
                root(0, 0)
                prep(1, 1)

                def step(b, s, prev, nxt, nxt2):
                    if nxt:
                        root(b + 1, 1 - s)
                    if nxt2:
                        prep(b + 2, s)
                    send(b, s)
                steps(pool, step)
                for s in range(2):
                    pool.wait_ge(sent[s], 16 * 2 * T * (B // 2))
                pool.wait_ge(S["wgt_in"], 16 * (KD + M))

            @block.vector
            def _(dve):
                dve.wait_ge(S["den_in"], 16 * B)
                nc.vector.reciprocal(den[:, :, :], den[:, :, :]).then_inc(S["den_done"], 1)

                def normalise(b, s):
                    dve.wait_ge(ld1[s], (b // 2 + 1) * 96)
                    if later(b, 2):
                        dve.wait_ge(S["ao_done"], (b - 1) * 2)
                    nc.vector.tensor_tensor(CT[:, s, :, :], num[:, s, :, :], inv[:, s, :, :], ALU.mult
                                            ).then_inc(S["ct"], 1)

                def residual(b, s):
                    dve.wait_ge(S["xb_done"], b + 1)
                    for m in range(2):
                        dve.wait_ge(S["ao_done"], b * 2 + (m + 1))
                        nc.vector.tensor_tensor(X_all[:, bass.ds(b * T + 2 * m, 2), :], ao[m][:, :, :],
                                                xb[:, s, 2 * m:2 * m + 2, :], ALU.add).then_inc(S["x1"], 1)
                    hold(dve, S["x1"], b * 2 + 2)
                    for t in range(T):
                        nc.vector.bn_stats(stats[:, s, t, :], X_all[:, b * T + t, :]).then_inc(S["stats"], 1)
                    hold(dve, S["stats"], b * T + T)
                    for t in range(T):
                        nc.vector.bn_aggr(mv[:, s, t, :], stats[:, s, t, :]).then_inc(S["mv"], 1)
                    dve.wait_ge(S["mv"], b * T + T)
                    nc.vector.tensor_scalar(var[:, s, :], mv[:, s, :, 1], EPS, None, ALU.add).then_inc(S["var"], 1)

                def modulate(b, s):
                    dve.wait_ge(S["rstd"], b + 1)
                    if later(b, 1):
                        dve.wait_ge(S["xm"], b)
                    for t in range(T):
                        nc.vector.tensor_scalar(xn[:, t, :], X_all[:, b * T + t, :], mv[:, s, t, 0:1],
                                                rstd[:, s, t:t + 1], ALU.subtract, ALU.mult).then_inc(S["xn"], 1)
                    dve.wait_ge(ld2[s], (b // 2 + 1) * 16)
                    dve.wait_ge(S["xn"], b * T + T)
                    if later(b, 1):
                        dve.wait_ge(S["h"], b)
                    nc.vector.tensor_tensor(xm[:, :, :], xn[:, :, :], mod2[:, s, 0, :].unsqueeze(1).to_broadcast(
                        [P, T, D]), ALU.mult).then_inc(S["xm"], 1)
                    dve.wait_ge(S["xm"], b + 1)
                    if later(b, 2):
                        dve.wait_ge(S["rows"], (b - 1) * (2 * T))
                    nc.vector.tensor_tensor(h[:, s, :, :], xm[:, :, :], mod2[:, s, 1, :].unsqueeze(1).to_broadcast(
                        [P, T, D]), ALU.add).then_inc(S["h"], 1)

                def route(b, s):
                    n = b * CHAIN
                    if later(b, 1):
                        dve.wait_ge(S["own"], n)
                        dve.wait_ge(S["weight"], b)
                    dve.wait_ge(S["exp"], b + 1)
                    nc.vector.tensor_scalar(e1[:, :, :], e[:, :, :], 1.0, None, ALU.add).then_inc(S["own"], 1)
                    dve.wait_ge(S["own"], n + 1)
                    nc.vector.reciprocal(score[:, :, :], e1[:, :, :]).then_inc(S["own"], 1)
                    dve.wait_ge(S["own"], n + 2)
                    nc.vector.tensor_tensor(biased[:, :, :], score[:, :, :], ebias[:, :].unsqueeze(1).to_broadcast(
                        [P, T, E]), ALU.add).then_inc(S["own"], 1)
                    hold(dve, S["own"], n + 3)
                    for t in range(T):
                        nc.vector.max(best[:, t, :], biased[:, t, :]).then_inc(S["own"], 1)
                    hold(dve, S["own"], n + 3 + T)
                    for t in range(T):
                        nc.vector.max_index(which[:, t, :], best[:, t, :], biased[:, t, :]).then_inc(S["own"], 1)
                    dve.wait_ge(S["own"], n + 3 + 2 * T)
                    nc.vector.tensor_copy(whichf[:, :, :], which[:, :, 0:2].rearrange("p t c -> p c t")
                                          ).then_inc(S["own"], 1)
                    dve.wait_ge(S["own"], n + 4 + 2 * T)
                    for c in range(2):
                        nc.vector.tensor_tensor(hot[:, c, :, :], iota_e[:, :].unsqueeze(1).to_broadcast([P, T, E]),
                                                whichf[:, c, :].unsqueeze(2).to_broadcast([P, T, E]),
                                                ALU.is_equal).then_inc(S["own"], 1)
                    dve.wait_ge(S["own"], n + 6 + 2 * T)
                    if later(b, 1):
                        dve.wait_ge(S["rank"], b)
                    nc.vector.tensor_tensor(picked[:, :, :], hot[:, 0, :, :], hot[:, 1, :, :], ALU.add
                                            ).then_inc(S["mask"], 1)
                    nc.vector.tensor_tensor(prod[:, :, :, :], hot[:, :, :, :], score[:, :, :].unsqueeze(1).to_broadcast(
                        [P, 2, T, E]), ALU.mult).then_inc(S["own"], 1)
                    if later(b, 2):
                        dve.wait_ge(S["rows"], (b - 1) * (2 * T))
                    dve.wait_ge(S["own"], n + 7 + 2 * T)
                    nc.vector.tensor_reduce(weight[:, s, :, :], prod[:, :, :, :], AX.X, ALU.add
                                            ).then_inc(S["weight"], 1)

                def locate(b, s):
                    n = b * CHAIN + 7 + 2 * T
                    dve.wait_ge(S["rank"], b + 1)
                    nc.vector.tensor_tensor(pos[:, :, :], rk[:, 0:T, :], base[:, s, :].unsqueeze(1).to_broadcast(
                        [P, T, E]), ALU.add).then_inc(S["own"], 1)
                    nc.vector.tensor_tensor(base[:, 1 - s, :], rk[:, T, :], base[:, s, :], ALU.add
                                            ).then_inc(S["own"], 1)
                    dve.wait_ge(S["own"], n + 2)
                    nc.vector.tensor_tensor(prod2[:, :, :, :], hot[:, :, :, :], pos[:, :, :].unsqueeze(1).to_broadcast(
                        [P, 2, T, E]), ALU.mult).then_inc(S["own"], 1)
                    dve.wait_ge(S["own"], n + 3)
                    nc.vector.tensor_reduce(posf[:, :, :], prod2[:, :, :, :], AX.X, ALU.add).then_inc(S["own"], 1)
                    if later(b, 2):
                        dve.wait_ge(sent[s], (b // 2) * (16 * 2 * T))
                    dve.wait_ge(S["own"], n + 4)
                    nc.vector.tensor_copy(place[:, s, :, :], posf[:, :, :]).then_inc(S["place"], 1)
                    nc.vector.tensor_copy(rows[:, s, :, :, D:ROWW].bitcast(U32), ids[:, s, :, :].unsqueeze(3)
                                          ).then_inc(S["ids"], 1)
                    if later(b, 1):
                        dve.wait_ge(S["ids"], b)
                    nc.vector.tensor_scalar(ids[:, 1 - s, :, :], ids[:, s, :, :], float(N), None, ALU.add
                                            ).then_inc(S["own"], 1)

                def finish(b, s):
                    dve.wait_ge(ld3[s], (b // 2 + 1) * 16)
                    if later(b, 1):
                        dve.wait_ge(S["x1s"], b)
                    for m in range(2):
                        dve.wait_ge(S["down"], b * 2 + (m + 1))
                        nc.vector.tensor_tensor(shared[:, 2 * m:2 * m + 2, :], ao[m][:, :, :],
                                                gb[:, s, :].unsqueeze(1).to_broadcast([P, 2, D]), ALU.mult
                                                ).then_inc(S["shared"], 1)
                    dve.wait_ge(S["shared"], b * 2 + 2)
                    nc.vector.tensor_tensor(X_all[:, bass.ds(b * T, T), :], X_all[:, bass.ds(b * T, T), :],
                                            shared[:, :, :], ALU.add).then_inc(S["x1s"], 1)

                dve.wait_ge(S["w_in"], 128)
                dve.wait_ge(S["set_up"], 5)
                normalise(0, 0)
                residual(0, 0)
                normalise(1, 1)
                modulate(0, 0)

                def step(b, s, prev, nxt, nxt2):
                    if prev:
                        finish(b - 1, 1 - s)
                    if nxt:
                        residual(b + 1, 1 - s)
                    route(b, s)
                    if nxt:
                        modulate(b + 1, 1 - s)
                    locate(b, s)
                    if nxt2:
                        normalise(b + 2, s)
                steps(dve, step)
                finish(B - 1, 1)
                dve.wait_ge(S["own"], B * CHAIN)
                nc.vector.tensor_copy(keep["ends"][:, :], base[:, 0, :]).then_inc(S["pad_done"], 1)

            @block.tensor
            def _(pe):
                def attention_out(b, s):
                    pe.wait_ge(S["ct"], b + 1)
                    pe.wait_ge(S["wog_done"], b + 1)
                    if later(b, 2):
                        pe.wait_ge(S["shared"], (b - 1) * 2)
                    for m in range(2):
                        for t2 in range(2):
                            t = 2 * m + t2
                            for k in range(KD):
                                last = nc.tensor.matmul(ao[m][:, t2, :], CT[:, s, k, t * P:(t + 1) * P],
                                                        Wog[:, s, k, :], start=(k == 0), stop=(k == KD - 1))
                        last.then_inc(S["ao_done"], 1)

                def turn(b, s):
                    pe.wait_ge(S["h"], b + 1)
                    for j in range(KD):
                        if later(b, 1):
                            pe.wait_ge(S["hT"], (b - 1) * KD + (j + 1))
                        for t in range(T):
                            last = nc.tensor.transpose(tp[j][:, t * P:(t + 1) * P], h[:, s, t, j * P:(j + 1) * P],
                                                       ident[:, :])
                        last.then_inc(S["tp"], 1)

                def router(b, s):
                    pe.wait_ge(S["hT"], b * KD + KD)
                    if later(b, 1):
                        pe.wait_ge(S["exp"], b)
                    for t in range(T):
                        for k in range(KD):
                            last = nc.tensor.matmul(lg[:, t, :], hT[:, s, k, t * P:(t + 1) * P], gateT[:, k, :],
                                                    start=(k == 0), stop=(k == KD - 1))
                    last.then_inc(S["logits"], 1)

                def rank(b, s):
                    pe.wait_ge(S["mask"], b + 1)
                    if later(b, 1):
                        pe.wait_ge(S["place"], b)
                    for t in range(T):
                        for j in range(t):
                            nc.tensor.matmul(rk[:, t, :], ones[:, :], picked[:, j, :], start=(j == 0), stop=False)
                        nc.tensor.matmul(rk[:, t, :], before[:, :], picked[:, t, :], start=(t == 0), stop=True)
                    for j in range(T):
                        last = nc.tensor.matmul(rk[:, T, :], ones[:, :], picked[:, j, :], start=(j == 0),
                                                stop=(j == T - 1))
                    last.then_inc(S["rank"], 1)

                def expand(b, s):
                    for m, (c, size) in enumerate(HT):
                        if later(b, 1) or m >= 2:
                            pe.wait_ge(S["relu"], b * M + (m - 1))
                        for k in range(KD):
                            last = nc.tensor.matmul(hp[(s + m) % 2][0:size, :], supT[:, k, c:c + size], hT[:, s, k, :],
                                                    start=(k == 0), stop=(k == KD - 1))
                        last.then_inc(S["hidden"], 1)

                def contract(b, s):
                    pe.wait_ge(S["hid"], b * M + M)
                    if not (isinstance(b, int) and b == B - 1):
                        pe.wait_ge(S["x1"], (b + 1) * 2 + 2)
                    for m in range(2):
                        for t2 in range(2):
                            t = 2 * m + t2
                            for j, (c, size) in enumerate(HT):
                                last = nc.tensor.matmul(ao[m][:, t2, :], hid[0:size, j, t * P:(t + 1) * P],
                                                        sdownT[0:size, j, :], start=(j == 0), stop=(j == M - 1))
                        last.then_inc(S["down"], 1)

                pe.wait_ge(S["w_in"], 128)
                pe.wait_ge(S["consts"], 1)
                attention_out(0, 0)
                turn(0, 0)

                def step(b, s, prev, nxt, nxt2):
                    router(b, s)
                    if nxt:
                        attention_out(b + 1, 1 - s)
                    expand(b, s)
                    rank(b, s)
                    if nxt:
                        turn(b + 1, 1 - s)
                    contract(b, s)
                steps(pe, step)

            @block.scalar
            def _(act):
                def turned(b, s):
                    for j in range(KD):
                        act.wait_ge(S["tp"], b * KD + (j + 1))
                        nc.scalar.copy(hT[:, s, j, :], tp[j][:, :]).then_inc(S["hT"], 1)

                def squares(b, s):
                    for m, (c, size) in enumerate(HT):
                        act.wait_ge(S["hidden"], b * M + (m + 1))
                        nc.scalar.activation(relu[0:size, m, :], hp[(s + m) % 2][0:size, :], ACT.Relu
                                             ).then_inc(S["relu"], 1)
                        act.wait_ge(S["relu"], b * M + (m + 1))
                        if m == 0 and later(b, 1):
                            act.wait_ge(S["down"], b * 2)
                        nc.scalar.activation(hid[0:size, m, :], relu[0:size, m, :], ACT.Square).then_inc(S["hid"], 1)

                def scale(b, s):
                    act.wait_ge(S["weight"], b + 1)
                    if later(b, 2):
                        act.wait_ge(sent[s], (b // 2) * (16 * 2 * T))
                    for c in range(2):
                        for t in range(T):
                            nc.scalar.mul(rows[:, s, c, t, 0:D], h[:, s, t, :], weight[:, s, c, t:t + 1]
                                          ).then_inc(S["rows"], 1)

                turned(0, 0)

                def step(b, s, prev, nxt, nxt2):
                    act.wait_ge(S["logits"], b + 1)
                    if later(b, 1):
                        act.wait_ge(S["own"], (b - 1) * CHAIN + 1)
                    nc.scalar.activation(e[:, :, :], lg[:, :, :], ACT.Exp, scale=-1.0).then_inc(S["exp"], 1)
                    squares(b, s)
                    if nxt:
                        turned(b + 1, 1 - s)
                    scale(b, s)
                steps(act, step)


def experts(nc, a, keep, dram, weights):
    up, down = weights
    M = len(HT)
    with ExitStack() as ctx:
        kit = Kit(nc, ctx, "exp_")
        start = kit.sb("start", [P, E])
        tile_no = kit.sb("tile_no", [P, TILES])
        count = kit.sb("count", [P, E])
        counti = kit.sb("counti", [P, E], I32)
        tilesi = kit.sb("tilesi", [P, E], I32)
        tiles = kit.sb("tiles", [P, E])
        unit = kit.sb("unit", [P, E])
        upto = kit.sb("upto", [P, E])
        past = kit.sb("past", [P, TILES, E])
        pastn = kit.sb("pastn", [P, TILES, E])
        whose = kit.sb("whose", [P, TILES])
        first = kit.sb("first", [P, TILES])
        inside = kit.sb("inside", [P, TILES])
        inside2 = kit.sb("inside2", [P, TILES])
        rowf = kit.sb("rowf", [P, TILES])
        row_of = kit.sb("row_of", [P, TILES], U32)
        expert_of = kit.sb("expert_of", [P, TILES], U32)
        endi = kit.sb("endi", [P, E], U32)
        padid = kit.sb("padid", [P, 2 * E * T])
        pad = kit.sb("pad", [P, 2 * E * T, ROWW], BF16)
        ident = kit.sb("identb", [P, P], BF16)
        rows = kit.sb("rows", [P, RING, T, ROWW], BF16)
        xT = kit.sb("xT", [P, RING, KD, BIG], BF16)
        relu = kit.sb("relu", [P, RING, M, BIG], BF16)
        hid = kit.sb("hid", [P, RING, M, BIG], BF16)
        ids = kit.sb("ids", [P, RING, T], U32)
        y = kit.sb("y", [P, RING, T, D], BF16)
        tp = [kit.ps(f"tp{i}", [P, KD, BIG], BF16) for i in range(2)]
        hp = [kit.ps(f"hp{m}", [P, BIG]) for m in range(M)]
        yp = [kit.ps(f"yp{i}", [P, 2, D]) for i in range(T // 2)]

        S = {n: kit.sem(n) for n in (
            "iotas", "own", "tables", "pads", "pad_set", "ends", "identb", "tp", "xT", "hidden", "relu", "hid", "yp",
            "y", "ids", "held")}
        rows_in = [kit.sem(f"rows_in{s}") for s in range(RING)]
        sent = [kit.sem(f"sent{s}") for s in range(RING)]

        def later(k, n):
            return not isinstance(k, int) or k >= n

        def hold(eng, sem, value):
            eng.wait_ge(sem, value)
            eng.sem_inc(S["held"], 1)

        def steps(eng, step):
            for k in range(RING):
                step(k, k, RING)
            with eng.Fori(1, TILES // RING - 1) as i:
                for r in range(RING):
                    step(i * RING + r, r, RING)
            for r in range(RING):
                step(TILES - RING + r, r, RING - 1 - r)

        with nc.Block() as block:

            @block.gpsimd
            def _(pool):
                def iota(out, pattern, base, channel):
                    nc.gpsimd.iota(out, pattern=pattern, base=base, channel_multiplier=channel,
                                   allow_small_or_imprecise_dtypes=True).then_inc(S["iotas"], 1)

                iota(start[:, :], [[CAP, E]], 0, 0)
                iota(tile_no[:, :], [[1, TILES]], 0, 0)
                iota(padid[:, :], [[P, 2 * E * T]], 2 * B * N, 1)
                nc.gpsimd.memset(unit[:, :], 1.0).then_inc(S["iotas"], 1)
                nc.gpsimd.memset(pad[:, :, 0:D], 0.0).then_inc(S["pad_set"], 1)

                def step(k, r, follow):
                    for t in range(T):
                        if t % 2 == 0:
                            hold(pool, S["y"], k * (T // 2) + (t // 2 + 1))
                        pool.indirect_dma_start(
                            out=dram["routed"], out_offset=bass.IndirectOffsetOnAxis(
                                ap=ids[:, r, t:t + 1], axis=0), in_=y[:, r, t, :], in_offset=None
                            ).then_inc(sent[r], 16)

                steps(pool, step)
                for r in range(RING):
                    pool.wait_ge(sent[r], 16 * T * (TILES // RING))

            @block.vector
            def _(dve):
                n = [0]

                def link(ins):
                    n[0] += 1
                    ins.then_inc(S["own"], 1)
                    dve.wait_ge(S["own"], n[0])

                v = nc.vector
                v.tensor_copy(ident[:, :], keep["ident"][:, :]).then_inc(S["identb"], 1)
                dve.wait_ge(S["iotas"], 4)
                v.tensor_copy(endi[:, :], keep["ends"][:, :]).then_inc(S["ends"], 1)
                v.tensor_copy(pad[:, :, D:ROWW].bitcast(U32), padid[:, :].unsqueeze(2)).then_inc(S["pad_set"], 1)
                link(v.tensor_tensor(count[:, :], keep["ends"][:, :], start[:, :], ALU.subtract))
                link(v.tensor_scalar(counti[:, :], count[:, :], float(BIG - 1), None, ALU.add))
                link(v.tensor_scalar(tilesi[:, :], counti[:, :], BIG.bit_length() - 1, None, ALU.arith_shift_right))
                link(v.tensor_copy(tiles[:, :], tilesi[:, :]))
                link(v.tensor_tensor_scan(upto[:, :], unit[:, :], tiles[:, :], 0.0, ALU.mult, ALU.add))
                link(v.tensor_tensor(past[:, :, :], tile_no[:, :].unsqueeze(2).to_broadcast([P, TILES, E]),
                                     upto[:, :].unsqueeze(1).to_broadcast([P, TILES, E]), ALU.is_ge))
                link(v.tensor_reduce(whose[:, :], past[:, :, :], AX.X, ALU.add))
                link(v.tensor_tensor(pastn[:, :, :], past[:, :, :],
                                     tiles[:, :].unsqueeze(1).to_broadcast([P, TILES, E]), ALU.mult))
                link(v.tensor_reduce(first[:, :], pastn[:, :, :], AX.X, ALU.add))
                link(v.tensor_tensor(inside[:, :], tile_no[:, :], first[:, :], ALU.subtract))
                link(v.tensor_scalar(inside2[:, :], inside[:, :], float(BIG), None, ALU.mult))
                link(v.scalar_tensor_tensor(out=rowf[:, :], in0=whose[:, :], scalar=float(CAP), in1=inside2[:, :],
                                            op0=ALU.mult, op1=ALU.add))
                v.tensor_copy(row_of[:, :], rowf[:, :]).then_inc(S["tables"], 1)
                v.tensor_scalar(expert_of[:, :], whose[:, :], float(E - 1), None, ALU.min).then_inc(S["tables"], 1)

                def turned(k, r):
                    dve.wait_ge(S["tp"], k + 1)
                    if later(k, RING):
                        dve.wait_ge(sent[r], (k // RING) * (16 * T))
                    v.tensor_copy(xT[:, r, :, :], tp[r % 2][:, :, :]).then_inc(S["xT"], 1)
                    v.tensor_copy(ids[:, r, :], rows[:, r, :, D:ROWW].bitcast(U32)).then_inc(S["ids"], 1)

                def square(k, r):
                    for m in range(M):
                        dve.wait_ge(S["relu"], k * M + (m + 1))
                        v.tensor_tensor(hid[:, r, m, :], relu[:, r, m, :], relu[:, r, m, :], ALU.mult
                                        ).then_inc(S["hid"], 1)

                def step(k, r, follow):
                    square(k, r)
                    if follow:
                        turned(k + 1, (r + 1) % RING)

                turned(0, 0)
                steps(dve, step)

            @block.tensor
            def _(pe):
                def turn(k, r):
                    pe.wait_ge(rows_in[r], (k // RING + 1) * 16)
                    if later(k, 2):
                        pe.wait_ge(S["xT"], k - 1)
                    for j in range(KD):
                        for t in range(T):
                            last = nc.tensor.transpose(tp[r % 2][:, j, t * P:(t + 1) * P],
                                                       rows[:, r, t, j * P:(j + 1) * P], ident[:, :])
                    last.then_inc(S["tp"], 1)

                def expand(k, r):
                    e = expert(k)
                    pe.wait_ge(S["xT"], k + 1)
                    for m in range(M):
                        if later(k, 1):
                            pe.wait_ge(S["relu"], (k - 1) * M + (m + 1))
                        for j in range(KD):
                            last = nc.tensor.matmul(hp[m][:, :], up[:, j, e, m * P:(m + 1) * P], xT[:, r, j, :],
                                                    start=(j == 0), stop=(j == KD - 1))
                        last.then_inc(S["hidden"], 1)

                def contract(k, r):
                    e = expert(k)
                    pe.wait_ge(S["hid"], k * M + M)
                    for i in range(T // 2):
                        if later(k, 1):
                            pe.wait_ge(S["y"], (k - 1) * (T // 2) + (i + 1))
                        for t2 in range(2):
                            t = 2 * i + t2
                            for m in range(M):
                                last = nc.tensor.matmul(yp[i][:, t2, :], hid[:, r, m, t * P:(t + 1) * P],
                                                        down[:, m, e, :], start=(m == 0), stop=(m == M - 1))
                        last.then_inc(S["yp"], 1)

                def expert(k):
                    return pe.value_load(expert_of[0:1, bass.ds(k, 1)], min_val=0, max_val=E - 1)

                pe.wait_ge(S["identb"], 1)
                pe.wait_ge(S["tables"], 2)
                turn(0, 0)

                def step(k, r, follow):
                    expand(k, r)
                    if follow:
                        turn(k + 1, (r + 1) % RING)
                    if later(k, 1):
                        contract(k - 1, (r - 1) % RING)
                steps(pe, step)
                contract(TILES - 1, RING - 1)

            @block.scalar
            def _(act):
                def load(k, r):
                    if later(k, RING):
                        act.wait_ge(S["tp"], k - RING + 1)
                        act.wait_ge(S["ids"], k - RING + 1)
                    row = act.value_load(row_of[0:1, bass.ds(k, 1)], min_val=0, max_val=E * CAP + (E - 1) * BIG)
                    act.dma_start(rows[:, r, :, :], dram["region"][bass.ds(row, BIG), :].rearrange(
                        "(t p) c -> p t c", p=P)).then_inc(rows_in[r], 16)

                def output(k, r):
                    for i in range(T // 2):
                        act.wait_ge(S["yp"], k * (T // 2) + (i + 1))
                        nc.scalar.copy(y[:, r, 2 * i:2 * i + 2, :], yp[i][:, :, :]).then_inc(S["y"], 1)

                def step(k, r, follow):
                    for m in range(M):
                        act.wait_ge(S["hidden"], k * M + (m + 1))
                        nc.scalar.activation(relu[:, r, m, :], hp[m][:, :], ACT.Relu).then_inc(S["relu"], 1)
                    if follow >= AHEAD:
                        load(k + AHEAD, (r + AHEAD) % RING)
                    if later(k, 1):
                        output(k - 1, (r - 1) % RING)

                act.wait_ge(S["ends"], 1)
                act.wait_ge(S["pad_set"], 2)
                for e in range(E):
                    end = act.value_load(endi[0:1, e:e + 1], min_val=e * CAP, max_val=(e + 1) * CAP - BIG)
                    act.dma_start(dram["region"][bass.ds(end, BIG), :].rearrange("(t p) c -> p t c", p=P),
                                  pad[:, e * T:(e + 1) * T, :]).then_inc(S["pads"], 16)
                act.dma_start(dram["region"][E * CAP:].rearrange("(j p) c -> p j c", p=P), pad[:, E * T:, :]
                              ).then_inc(S["pads"], 16)
                act.wait_ge(S["tables"], 2)
                act.wait_ge(S["pads"], 16 * (E + 1))
                for k in range(AHEAD):
                    load(k, k)
                steps(act, step)
                output(TILES - 1, RING - 1)


def merge(nc, keep, dram, X_all, out):
    with ExitStack() as ctx:
        kit = Kit(nc, ctx, "merge_")
        r = kit.sb("r", [P, 2, 2, T, D], BF16)
        gb = kit.sb("gb", [P, 2, D])
        both = kit.sb("both", [P, 2, T, D])
        gated = kit.sb("gated", [P, 2, T, D])
        o = kit.sb("o", [P, 2, T, D])
        r_in = [kit.sem(f"r_in{s}") for s in range(2)]
        stored = [kit.sem(f"stored{s}") for s in range(2)]
        summed, gate, done = kit.sem("summed"), kit.sem("gate"), kit.sem("done")

        def later(b, k):
            return not isinstance(b, int) or b >= k

        with nc.Block() as block:

            @block.sync
            def _(sp):
                def load(b, s):
                    if later(b, 2):
                        sp.wait_ge(gate, b - 1)
                    for c in range(2):
                        sp.dma_start(r[:, s, c, :, :], dram["routed"][bass.ds(b * N + c * (B * N), N), :].rearrange(
                            "(t p) d -> p t d", p=P)).then_inc(r_in[s], 16)
                    sp.dma_start(gb[:, s, :], dram["rows"][b, 1:2, :].partition_broadcast(P)).then_inc(r_in[s], 16)
                load(0, 0)
                load(1, 1)
                pairs(sp, 2, B, load)

            @block.vector
            def _(dve):
                def step(b, s):
                    dve.wait_ge(r_in[s], (b // 2 + 1) * 48)
                    if later(b, 2):
                        dve.wait_ge(gate, b - 1)
                    nc.vector.tensor_tensor(both[:, s, :, :], r[:, s, 0, :, :], r[:, s, 1, :, :], ALU.add
                                            ).then_inc(summed, 1)
                    dve.wait_ge(summed, b + 1)
                    if later(b, 2):
                        dve.wait_ge(done, b - 1)
                    nc.vector.tensor_tensor(gated[:, s, :, :], both[:, s, :, :], gb[:, s, :].unsqueeze(1).to_broadcast(
                        [P, T, D]), ALU.mult).then_inc(gate, 1)
                step(0, 0)
                step(1, 1)
                pairs(dve, 2, B, step)

            @block.gpsimd
            def _(pool):
                def step(b, s):
                    pool.wait_ge(gate, b + 1)
                    if later(b, 2):
                        pool.wait_ge(stored[s], (b // 2) * 16)
                    nc.gpsimd.tensor_tensor(o[:, s, :, :], X_all[:, bass.ds(b * T, T), :], gated[:, s, :, :], ALU.add
                                            ).then_inc(done, 1)
                step(0, 0)
                step(1, 1)
                pairs(pool, 2, B, step)

            @block.scalar
            def _(act):
                def store(b, s):
                    act.wait_ge(done, b + 1)
                    act.dma_start(out[b].rearrange("(t p) d -> p t d", p=P), o[:, s, :, :]).then_inc(stored[s], 16)
                pairs(act, 0, B, store)
                for s in range(2):
                    act.wait_ge(stored[s], 16 * (B // 2))


def program(nc, a, out, stages=5):
    def scratch(name, shape, dt=F32):
        return nc.dram_tensor(name, shape, dt, kind="Internal").ap()

    dram = {
        "table": scratch("table_d", [HP, P, 2, N]),
        "rows": scratch("rows_d", [B, 4, D]),
        "q": scratch("q_d", [HP, B, PARTS, 32, N], BF16),
        "k": scratch("k_d", [HP, B, PARTS, 32, N], BF16),
        "ctx": scratch("ctx_d", [B, HP, 4 * HD, N]),
        "inv": scratch("inv_d", [B, H * N]),
        "region": scratch("region_d", [E * CAP + E * BIG, ROWW], BF16),
        "routed": scratch("routed_d", [2 * B * N + 2 * E * BIG, D], BF16),
    }
    with ExitStack() as ctx:
        kit = Kit(nc, ctx, "")
        keep = {"ident": kit.sb("ident", [P, P]), "modT": kit.sb("modT", [P, 2, KD, B]), "ends": kit.sb("ends", [P, E])}
        prepare(nc, a, keep, dram)
        with ExitStack() as inner:
            V_all = Kit(nc, inner, "").sb("V_all", [P, STEPS, T * 2 * HD])
            project(nc, a, keep, dram, V_all)
            if stages >= 3:
                attend(nc, a, keep, dram, V_all)
        if stages >= 4:
            X_all = kit.sb("X_all", [P, B * T, D])
            up = kit.sb("up", [P, KD, E, len(HT) * P], BF16)
            down = kit.sb("down", [P, len(HT), E, D], BF16)
            feed(nc, a, keep, dram, X_all, (up, down))
            if stages >= 5:
                experts(nc, a, keep, dram, (up, down))
                merge(nc, keep, dram, X_all, out)


def laid_out(i):
    import numpy as np
    def pair_order(w):
        return w.reshape(D, HP, 2, HD).transpose(0, 1, 3, 2).reshape(D, D)
    r = {
        "x": i["L0_attn_x"], "Wq": pair_order(i["L0_attn_Wq"]), "Wk": pair_order(i["L0_attn_Wk"]),
        "Wv": i["L0_attn_Wv"], "Wo": i["L0_attn_Wo"], "bo": i["L0_attn_bo"], "w": i["L0_attn_w"], "v": i["L0_attn_v"],
        "gateT": i["L0_ffn_gate_w"].T, "bias": i["L0_ffn_expert_bias"],
        "upT": i["L0_ffn_w_up"].transpose(2, 0, 1), "downT": i["L0_ffn_w_down"].transpose(2, 0, 1),
        "supT": i["L0_ffn_shared_w_up"].T, "sdownT": i["L0_ffn_shared_w_down"].T,
        "cT": i["L0_c"].T, "wmod": i["L0_wmod"],
    }
    return {k: np.ascontiguousarray(v) for k, v in r.items()}


def kernel(**inputs):
    import numpy as np
    import concourse.bacc as bacc
    from concourse.bass_utils import run_bass_kernel_spmd

    nc = bacc.Bacc("TRN2", target_bir_lowering=False, num_devices=1)
    arrays = laid_out({k: np.asarray(v) for k, v in inputs.items()})
    aps = {k: nc.dram_tensor("in_" + k, v.shape, mybir.dt.from_np(v.dtype), kind="ExternalInput").ap()
           for k, v in arrays.items()}
    out = nc.dram_tensor("out", (B, N, D), F32, kind="ExternalOutput").ap()
    program(nc, aps, out)
    r = run_bass_kernel_spmd(nc, [{"in_" + k: v for k, v in arrays.items()}], core_ids=[0])
    return r.results[0]["out"]
```

```python
from contextlib import ExitStack

import concourse.bass as bass
from concourse import mybir
from concourse.alu_op_type import AluOpType as ALU

ACT = mybir.ActivationFunctionType
F32 = mybir.dt.float32
BF16 = mybir.dt.bfloat16
U32 = mybir.dt.uint32
I32 = mybir.dt.int32
AX = mybir.AxisListType

P = 128
B, N, D = 16, 512, 256
H, HD = 16, 16
E, HID = 8, 352
T = N // P
KD = D // P
HP = H // 2
STEPS = HP * B
PARTS = 3
STACK = 96
EPS = 1e-5
SA, CA, GA, SB, CB, GB = range(6)
ROWW = D + 2
BIG = T * P
CAP = B * N + BIG
TILES = 2 * B * N // BIG + E - 1
CHAIN = 12 + 2 * T
RING = 4
AHEAD = 3
HT = [(0, 128), (128, 128), (256, 96)]


def pairs(eng, first, last, step):
    n = (last - first) // 2
    if n:
        with eng.Fori(0, n) as i:
            for u in range(2):
                step(i * 2 + (first + u), (first + u) % 2)
    if (last - first) % 2:
        step(last - 1, (last - 1) % 2)


class Kit:

    def __init__(self, nc, ctx, stage):
        self.nc, self.ctx, self.stage = nc, ctx, stage

    def sb(self, name, shape, dt=F32):
        return self.ctx.enter_context(self.nc.sbuf_tensor(self.stage + name, shape, dt))

    def ps(self, name, shape, dt=F32):
        return self.ctx.enter_context(self.nc.psum_tensor(self.stage + name, shape, dt))

    def sem(self, name):
        return self.ctx.enter_context(self.nc.semaphore(self.stage + name))


def prepare(nc, a, keep, dram):
    with ExitStack() as ctx:
        kit = Kit(nc, ctx, "prep_")
        cT = kit.sb("cT", [P, KD, B])
        wmod = kit.sb("wmod", [P, KD, 6 * D])
        e = kit.sb("e", [P, KD, B])
        e1 = kit.sb("e1", [P, KD, B])
        er = kit.sb("er", [P, KD, B])
        sT = kit.sb("sT", [P, KD, B])
        wrow = kit.sb("wrow", [P, H])
        ev = kit.sb("ev", [P, H])
        vrow, nw, top, dpos = keep["vrow"], keep["nw"], keep["top"], keep["dpos"]
        dist = kit.sb("dist", [P, N])
        g = kit.sb("g", [B, 2, D])
        gneg = kit.sb("gneg", [B, 2, D])
        gmag = kit.sb("gmag", [B, 2, D])
        gsgn = kit.sb("gsgn", [B, 2, D])
        gsg2 = kit.sb("gsg2", [B, 2, D])
        gate, mod2 = keep["gate"], keep["mod2"]
        ones = kit.sb("ones", [P, P])
        padid, pad = keep["padid"], keep["pad"]
        modT_ps = kit.ps("modT_ps", [P, 2, KD, B])
        mod2_ps = kit.ps("mod2_ps", [B, 2, D])
        gate_ps = kit.ps("gate_ps", [B, 2, D])

        loaded = kit.sem("loaded")
        wv_in = kit.sem("wv_in")
        exp_c = kit.sem("exp_c")
        silu = kit.sem("silu")
        mod_ps = kit.sem("mod_ps")
        gate_done = kit.sem("gate_done")
        dist_done = kit.sem("dist_done")
        ev_done = kit.sem("ev_done")
        ones_done = kit.sem("ones_done")
        MODS = [SA, CA]

        with nc.Block() as block:

            @block.sync
            def _(sp):
                sp.dma_start(cT[:, :, :], a["cT"].rearrange("(k p) b -> p k b", p=P)).then_inc(loaded, 16)
                sp.dma_start(wmod[:, :, :], a["wmod"].rearrange("(k p) n -> p k n", p=P)).then_inc(loaded, 16)
                sp.dma_start(wrow[:, :], a["w"].unsqueeze(0).partition_broadcast(P)).then_inc(wv_in, 16)
                sp.dma_start(vrow[:, :], a["v"].unsqueeze(0).partition_broadcast(P)).then_inc(wv_in, 16)
                for n, tile in keep["w"].items():
                    sp.dma_start(tile[:, :, :], a[n].rearrange("(k p) n -> p k n", p=P)).then_inc(keep["w_in"], 16)
                for b in range(2):
                    sp.dma_start(keep["x"][:, b, :, :], a["x"][b].rearrange("(t p) d -> p t d", p=P)
                                 ).then_inc(keep["x_in"][b], 16)
                sp.wait_ge(gate_done, 3)
                sp.dma_start(dram["rows"][:, 0:2, :], gate[:, :, :]).then_inc(keep["rows_out"], 16)
                sp.dma_start(dram["rows"][:, 2:4, :], mod2[:, :, :]).then_inc(keep["rows_out"], 16)

            @block.scalar
            def _(act):
                act.wait_ge(loaded, 32)
                nc.scalar.activation(e[:, :, :], cT[:, :, :], ACT.Exp, scale=-1.0).then_inc(exp_c, 1)
                act.wait_ge(wv_in, 32)
                nc.scalar.activation(ev[:, :], vrow[:, :], ACT.Exp).then_inc(ev_done, 1)

            @block.gpsimd
            def _(pool):
                nc.gpsimd.iota(dist[:, :], pattern=[[-1, N]], base=(T - 1) * P, channel_multiplier=1,
                               allow_small_or_imprecise_dtypes=True).then_inc(dist_done, 1)
                nc.gpsimd.memset(ones[:, :], 1.0).then_inc(ones_done, 1)
                pool.wait_ge(ones_done, 1)
                nc.gpsimd.affine_select(keep["ident"][:, :], ones[:, :], pattern=[[-1, P]], compare_op=ALU.is_equal,
                                        fill=0.0, base=0, channel_multiplier=1)
                nc.gpsimd.iota(padid[:, :], pattern=[[P, 2 * E * T]], base=2 * B * N, channel_multiplier=1,
                               allow_small_or_imprecise_dtypes=True)
                nc.gpsimd.memset(pad[:, :, 0:D], 0.0)

            @block.tensor
            def _(pe):
                pe.wait_ge(silu, 1)
                for c, chunk in enumerate(MODS):
                    for j in range(KD):
                        for k in range(KD):
                            col = chunk * D + j * P
                            nc.tensor.matmul(modT_ps[:, c, j, :], wmod[:, k, col:col + P], sT[:, k, :],
                                             start=(k == 0), stop=(k == KD - 1))
                for c, chunk in enumerate([GA, GB, CB, SB]):
                    rows_ps = gate_ps if c < 2 else mod2_ps
                    for k in range(KD):
                        last = nc.tensor.matmul(rows_ps[:, c % 2, :], sT[:, k, :], wmod[:, k, chunk * D:(chunk + 1) * D],
                                                start=(k == 0), stop=(k == KD - 1))
                last.then_inc(mod_ps, 1)

            @block.vector
            def _(dve):
                step = [0]

                def after(ins, sem):
                    step[0] += 1
                    ins.then_inc(sem, 1)
                    dve.wait_ge(sem, step[0])

                own = kit.sem("own")
                dve.wait_ge(exp_c, 1)
                after(nc.vector.tensor_scalar(e1[:, :, :], e[:, :, :], 1.0, None, ALU.add), own)
                after(nc.vector.reciprocal(er[:, :, :], e1[:, :, :]), own)
                nc.vector.tensor_tensor(sT[:, :, :], cT[:, :, :], er[:, :, :], ALU.mult).then_inc(silu, 1)
                dve.wait_ge(wv_in, 32)
                nc.vector.tensor_scalar(nw[:, :], wrow[:, :], -1.0, None, ALU.mult)
                dve.wait_ge(dist_done, 1)
                nc.vector.tensor_scalar(dpos[:, :], dist[:, :], 0.0, None, ALU.max)
                dve.wait_ge(ev_done, 1)
                nc.vector.tensor_scalar(top[:, :], ev[:, :], 1.0, HD ** -0.5, ALU.add, ALU.mult)
                dve.wait_ge(mod_ps, 1)
                for c in range(2):
                    nc.vector.tensor_scalar(mod2[:, c, :], mod2_ps[:, c, :], 1.0 - c, None, ALU.add
                                            ).then_inc(gate_done, 1)
                for c in range(2):
                    nc.vector.tensor_scalar(keep["modT"][:, c, :, :], modT_ps[:, c, :, :], float(c % 2), None, ALU.add)
                after(nc.vector.tensor_copy(g[:, :, :], gate_ps[:, :, :]), own)
                after(nc.vector.tensor_scalar(gneg[:, :, :], g[:, :, :], -1.0, 0.25, ALU.mult, ALU.max), own)
                after(nc.vector.tensor_tensor(gmag[:, :, :], g[:, :, :], gneg[:, :, :], ALU.max), own)
                after(nc.vector.tensor_scalar(gsgn[:, :, :], g[:, :, :], 0.0, 2.0, ALU.is_ge, ALU.mult), own)
                after(nc.vector.tensor_scalar(gsg2[:, :, :], gsgn[:, :, :], 1.0, None, ALU.subtract), own)
                nc.vector.tensor_tensor(gate[:, :, :], gmag[:, :, :], gsg2[:, :, :], ALU.mult).then_inc(gate_done, 1)


def project(nc, a, keep, dram, V_all):
    assert H == B
    with ExitStack() as ctx:
        kit = Kit(nc, ctx, "proj_")
        ident, modT = keep["ident"], keep["modT"]
        w, x, w_in, x_in = keep["w"], keep["x"], keep["w_in"], keep["x_in"]
        stats = kit.sb("stats", [P, 2, T, 6])
        mv = kit.sb("mv", [P, 2, T, 2])
        var = kit.sb("var", [P, 2, T])
        rstd = kit.sb("rstd", [P, 2, T])
        xn = kit.sb("xn", [P, 2, T, D])
        hT = kit.sb("hT", [P, 2, KD, N])
        rest = kit.sb("rest", [P, 2 * KD, N])
        part = kit.sb("part", [P, 2, 2 * KD, PARTS, N], BF16)
        half = kit.sb("half", [P, T])
        vrow, nw, top, dpos = keep["vrow"], keep["nw"], keep["top"], keep["dpos"]
        den = kit.sb("den", [P, 2, N])
        den1 = kit.sb("den1", [P, N])
        inv = kit.sb("inv", [P, N])
        raw = kit.sb("raw", [P, 2, N])
        tab = kit.sb("tab", [P, 2, N])
        tp = [kit.ps(f"tp{j}", [P, N]) for j in range(KD)]
        qk = [kit.ps(f"qk{m}", [P, N]) for m in range(2 * KD)]
        vp = [kit.ps(f"vp{m}", [P, 2, D]) for m in range(2)]

        half_set = kit.sem("half_set")
        stats_done = kit.sem("stats_done")
        mv_done = kit.sem("mv_done")
        held = kit.sem("held")
        var_done = kit.sem("var_done")
        rstd_done = kit.sem("rstd_done")
        xn_done = kit.sem("xn_done")
        tp_done = kit.sem("tp_done")
        hT_done = kit.sem("hT_done")
        qk_done = kit.sem("qk_done")
        vp_done = kit.sem("vp_done")
        v_out = kit.sem("v_out")
        part1 = kit.sem("part1")
        rest_done = kit.sem("rest_done")
        part2 = kit.sem("part2")
        part3 = kit.sem("part3")
        stored = [kit.sem(f"stored{s}") for s in range(2)]
        pad_set = kit.sem("pad_set")
        pad_out = kit.sem("pad_out")
        den_done = kit.sem("den_done")
        den1_done = kit.sem("den1_done")
        inv_done = kit.sem("inv_done")
        raw_done = kit.sem("raw_done")
        tab_done = kit.sem("tab_done")
        tab_out = [kit.sem(f"tab_out{s}") for s in range(2)]
        M = 2 * KD
        slot1 = [2, 2, 0, 0]
        slot3 = [0, 0, 2, 2]

        def hold(eng, sem, value):
            eng.wait_ge(sem, value)
            eng.sem_inc(held, 1)

        with nc.Block() as block:

            @block.sync
            def _(sp):
                def load(b, s):
                    sp.wait_ge(xn_done, b * T - T)
                    sp.dma_start(x[:, s, :, :], a["x"][b].rearrange("(t p) d -> p t d", p=P)).then_inc(x_in[s], 16)

                def store(b, s):
                    for m in range(M):
                        sp.wait_ge(part3, b * M + (m + 1))
                        dst = dram["q" if m < KD else "k"]
                        g = HP // KD
                        for r in range(PARTS):
                            sp.dma_start(dst[(m % KD) * g:(m % KD + 1) * g, b, r],
                                         part[:, s, m, r, :]).then_inc(stored[s], 16)

                sp.wait_ge(pad_set, 1)
                sp.dma_start(dram["region"][E * CAP:].rearrange("(j p) c -> p j c", p=P), keep["pad"][:, :, :]
                             ).then_inc(pad_out, 16)

                def store_table(h, s):
                    sp.wait_ge(tab_done, h + 1)
                    sp.dma_start(dram["table"][h // 2, :, s, :], tab[:, s, :]).then_inc(tab_out[s], 16)

                def step(b, s):
                    load(b + 2, s)
                    store(b, s)
                    store_table(b, s)
                pairs(sp, 0, B - 2, step)
                for b in range(B - 2, B):
                    store(b, b % 2)
                    store_table(b, b % 2)
                sp.wait_ge(pad_out, 16)
                sp.wait_ge(keep["rows_out"], 32)
                for s in range(2):
                    sp.wait_ge(tab_out[s], 16 * (H // 2))
                    sp.wait_ge(stored[s], 16 * (B // 2) * M * PARTS)

            @block.gpsimd
            def _(pool):
                nc.gpsimd.memset(half[:, :], -0.5).then_inc(half_set, 1)
                pool.wait_ge(half_set, 1)

                def root(b, s):
                    pool.wait_ge(var_done, b + 1)
                    nc.gpsimd.tensor_tensor(rstd[:, s, :], var[:, s, :], half[:, :], ALU.pow).then_inc(rstd_done, 1)

                def step(b, s, ahead=True):
                    if ahead:
                        root(b + 1, 1 - s)
                    for m in range(M):
                        pool.wait_ge(part2, b * M + (m + 1))
                        nc.gpsimd.tensor_tensor(part[:, s, m, slot3[m], :], rest[:, m, :], part[:, s, m, 1, :],
                                                ALU.subtract).then_inc(part3, 1)
                    table(b, s)

                def table(h, s):
                    hold(pool, raw_done, h + 1)
                    if not isinstance(h, int) or h >= 2:
                        hold(pool, tab_out[s], (h // 2) * 16)
                    nc.gpsimd.affine_select(tab[:, s, :], raw[:, s, :], pattern=[[-1, N]], compare_op=ALU.is_ge,
                                            fill=0.0, base=(T - 1) * P, channel_multiplier=1).then_inc(tab_done, 1)

                root(0, 0)
                step(0, 0)
                step(1, 1)
                pairs(pool, 2, B - 1, step)
                step(B - 1, (B - 1) % 2, ahead=False)

            @block.vector
            def _(dve):
                def norm(b, s):
                    dve.wait_ge(x_in[s], (b // 2 + 1) * 16)
                    for t in range(T):
                        nc.vector.bn_stats(stats[:, s, t, :], x[:, s, t, :]).then_inc(stats_done, 1)
                    hold(dve, stats_done, b * T + T)
                    for t in range(T):
                        nc.vector.bn_aggr(mv[:, s, t, :], stats[:, s, t, :]).then_inc(mv_done, 1)
                    dve.wait_ge(mv_done, b * T + T)
                    nc.vector.tensor_scalar(var[:, s, :], mv[:, s, :, 1], EPS, None, ALU.add).then_inc(var_done, 1)

                def scale(b, s):
                    dve.wait_ge(rstd_done, b + 1)
                    for t in range(T):
                        last = nc.vector.tensor_scalar(xn[:, s, t, :], x[:, s, t, :], mv[:, s, t, 0:1],
                                                       rstd[:, s, t:t + 1], ALU.subtract, ALU.mult)
                        last.then_inc(xn_done, 1)

                def split(b, s, m):
                    dve.wait_ge(part1, b * M + (m + 1))
                    if not isinstance(b, int) or b:
                        dve.wait_ge(part3, (b - 1) * M + (m + 1))
                    nc.vector.tensor_tensor(rest[:, m, :], qk[m][:, :], part[:, s, m, slot1[m], :],
                                            ALU.subtract).then_inc(rest_done, 1)

                def round2(b, s, m):
                    dve.wait_ge(rest_done, b * M + (m + 1))
                    nc.vector.tensor_copy(part[:, s, m, 1, :], rest[:, m, :]).then_inc(part2, 1)

                def step(b, s, ahead=True):
                    if ahead:
                        norm(b + 1, 1 - s)
                    split(b, s, 0)
                    split(b, s, 1)
                    if ahead:
                        scale(b + 1, 1 - s)
                    round2(b, s, 0)
                    split(b, s, 2)
                    round2(b, s, 1)
                    split(b, s, 3)
                    round2(b, s, 2)
                    round2(b, s, 3)
                    table(b, s)

                def table(h, s):
                    dve.wait_ge(den_done, h + 1)
                    if not isinstance(h, int) or h:
                        dve.wait_ge(raw_done, h)
                    nc.vector.tensor_scalar(den1[:, :], den[:, s, :], 1.0, None, ALU.add).then_inc(den1_done, 1)
                    dve.wait_ge(den1_done, h + 1)
                    nc.vector.reciprocal(inv[:, :], den1[:, :]).then_inc(inv_done, 1)
                    dve.wait_ge(inv_done, h + 1)
                    if not isinstance(h, int) or h >= 2:
                        dve.wait_ge(tab_done, h - 1)
                    nc.vector.tensor_scalar(raw[:, s, :], inv[:, :], top[:, bass.ds(h, 1)], None,
                                            ALU.mult).then_inc(raw_done, 1)

                norm(0, 0)
                nc.vector.tensor_copy(keep["pad"][:, :, D:ROWW].bitcast(U32), keep["padid"][:, :].unsqueeze(2)
                                      ).then_inc(pad_set, 1)
                scale(0, 0)
                step(0, 0)
                step(1, 1)
                pairs(dve, 2, B - 1, step)
                step(B - 1, (B - 1) % 2, ahead=False)

            @block.tensor
            def _(pe):
                def turn(b, s):
                    pe.wait_ge(xn_done, b * T + T)
                    for j in range(KD):
                        if not isinstance(b, int) or b:
                            pe.wait_ge(hT_done, (b - 1) * KD + (j + 1))
                        for t in range(T):
                            last = nc.tensor.transpose(tp[j][:, t * P:(t + 1) * P], xn[:, s, t, j * P:(j + 1) * P],
                                                       ident[:, :])
                        last.then_inc(tp_done, 1)

                def project_qk(b, s):
                    pe.wait_ge(hT_done, b * KD + KD)
                    for m in range(M):
                        if not isinstance(b, int) or b:
                            pe.wait_ge(rest_done, (b - 1) * M + (m + 1))
                        src = w["Wq"] if m < KD else w["Wk"]
                        for k in range(KD):
                            last = nc.tensor.matmul(qk[m][:, :], src[:, k, (m % KD) * P:(m % KD + 1) * P],
                                                    hT[:, s, k, :], start=(k == 0), stop=(k == KD - 1))
                        last.then_inc(qk_done, 1)

                def project_v(b, s):
                    for m in range(2):
                        if not isinstance(b, int) or b:
                            pe.wait_ge(v_out, (b - 1) * 2 + (m + 1))
                        for t2 in range(2):
                            t = 2 * m + t2
                            for k in range(KD):
                                last = nc.tensor.matmul(vp[m][:, t2, :], hT[:, s, k, t * P:(t + 1) * P],
                                                        w["Wv"][:, k, :], start=(k == 0), stop=(k == KD - 1))
                        last.then_inc(vp_done, 1)

                def step(b, s, ahead=True):
                    project_qk(b, s)
                    if ahead:
                        turn(b + 1, 1 - s)
                    project_v(b, s)

                pe.wait_ge(w_in, 48)
                turn(0, 0)
                step(0, 0)
                pairs(pe, 1, B - 1, step)
                step(B - 1, (B - 1) % 2, ahead=False)

            @block.scalar
            def _(act):
                def modulate(b, s):
                    for j in range(KD):
                        act.wait_ge(tp_done, b * KD + (j + 1))
                        if not isinstance(b, int) or b >= 2:
                            act.wait_ge(vp_done, (b - 2) * 2 + 2)
                        nc.scalar.activation(hT[:, s, j, :], tp[j][:, :], ACT.Identity,
                                             bias=modT[:, 0, j, bass.ds(b, 1)],
                                             scale=modT[:, 1, j, bass.ds(b, 1)]).then_inc(hT_done, 1)

                def first(b, s, m):
                    act.wait_ge(qk_done, b * M + (m + 1))
                    if not isinstance(b, int) or b >= 2:
                        act.wait_ge(stored[s], (b // 2) * (16 * M * PARTS))
                    nc.scalar.copy(part[:, s, m, slot1[m], :], qk[m][:, :]).then_inc(part1, 1)

                def values(b, m):
                    act.wait_ge(vp_done, b * 2 + (m + 1))
                    for t2 in range(2):
                        last = nc.scalar.copy(
                            V_all[:, :, :].rearrange("p (g b) c -> p g b c", b=B)
                            [:, :, b, (2 * m + t2) * 32:(2 * m + t2) * 32 + 32],
                            vp[m][:, t2, :].rearrange("p (g c) -> p g c", c=32))
                    last.then_inc(v_out, 1)

                def step(b, s, ahead=True):
                    for m in range(M):
                        first(b, s, m)
                    if not isinstance(b, int) or b >= 2:
                        act.wait_ge(den1_done, b - 1)
                    nc.scalar.activation(den[:, s, :], dpos[:, :], ACT.Exp, bias=vrow[:, bass.ds(b, 1)],
                                         scale=nw[:, bass.ds(b, 1)]).then_inc(den_done, 1)
                    if ahead:
                        modulate(b + 1, 1 - s)
                    for m in range(2):
                        values(b, m)

                modulate(0, 0)
                step(0, 0)
                step(1, 1)
                pairs(act, 2, B - 1, step)
                step(B - 1, (B - 1) % 2, ahead=False)


def attend(nc, a, keep, dram, V_all):
    units = [[(0, 3, 0)], [(0, 0, 0), (0, 2, P)], [(1, 3, 0)], [(1, 0, 0), (1, 2, P)], [(0, 1, 0), (1, 1, 2 * P)]]
    NU = len(units)
    WHEN = [[], [], [0], [1], [2, 3]]
    LEAD = 4
    NX = sum(len(u) for u in units)
    ROW = N + P
    with ExitStack() as ctx:
        kit = Kit(nc, ctx, "att_")
        ident = keep["ident"]
        Q = kit.sb("Q", [STACK, 2, 2 * N], BF16)
        K = kit.sb("K", [STACK, 2, 2 * N], BF16)
        table = kit.sb("table", [P, 2, 2, N])
        V = kit.sb("V", [P, 2, T, 2, 2 * HD])
        scaled = kit.sb("scaled", [P, NU, N])
        top = kit.sb("top", [P, NU, 2])
        shifted = kit.sb("shifted", [P, NU, N])
        prob = kit.sb("prob", [P, 2, 2, T * ROW])
        ctxT = kit.sb("ctxT", [4 * HD, 2, N])
        s_ps = [kit.ps(f"s{i}", [P, N]) for i in range(NU)]
        t_ps = [kit.ps(f"t{i}", [P, N]) for i in range(2)]
        o_ps = kit.ps("o", [4 * HD, N])

        q_in = [kit.sem(f"q_in{s}") for s in range(2)]
        k_in = [kit.sem(f"k_in{s}") for s in range(2)]
        table_in = [kit.sem(f"table_in{s}") for s in range(2)]
        ones_set = kit.sem("ones_set")
        v_ready = kit.sem("v_ready")
        scores = kit.sem("scores")
        maxed = kit.sem("maxed")
        relued = kit.sem("relued")
        turned = kit.sem("turned")
        exped = kit.sem("exped")
        masked = kit.sem("masked")
        summed = kit.sem("summed")
        copied = kit.sem("copied")
        stored = [kit.sem(f"stored{s}") for s in range(2)]
        held = kit.sem("held")

        def hold(eng, sem, value):
            eng.wait_ge(sem, value)
            eng.sem_inc(held, 1)

        def bank(banks, s, u):
            return banks[(s + u) % 2]

        with nc.Block() as block:

            @block.sync
            def _(sp):
                def load(n, s):
                    if not isinstance(n, int) or n >= 2:
                        sp.wait_ge(scores, (n - 1) * NU)
                    hp, b = n // B, n % B
                    for name, buf, sem, mid, low in (("q", Q, q_in, 1, 2), ("k", K, k_in, 0, 0)):
                        src = dram[name]
                        sp.dma_start(buf[0:48, s, :], src[hp, b].rearrange("r (d h) n -> (r d) (h n)", h=2)
                                     ).then_inc(sem[s], 16)
                        sp.dma_start(buf[48:80, s, :], src[hp, b, mid:mid + 2].rearrange(
                            "r (d h) n -> (r d) (h n)", h=2)).then_inc(sem[s], 16)
                        sp.dma_start(buf[80:96, s, :], src[hp, b, low].rearrange("(d h) n -> d (h n)", h=2)
                                     ).then_inc(sem[s], 16)

                def load_table(hp, s):
                    if not isinstance(hp, int) or hp >= 2:
                        sp.wait_ge(maxed, (hp - 1) * (B * NU))
                    sp.dma_start(table[:, s, :, :], dram["table"][hp]).then_inc(table_in[s], 16)

                load_table(0, 0)
                load(0, 0)
                load(1, 1)
                load_table(1, 1)
                pairs(sp, 2, B, load)
                with sp.Fori(0, (HP - 2) // 2) as g:
                    for half in range(2):
                        hp = g * 2 + (1 + half)
                        load(hp * B, 0)
                        load(hp * B + 1, 1)
                        load_table(hp + 1, half)
                        with sp.Fori(1, B // 2) as i:
                            load(hp * B + i * 2, 0)
                            load(hp * B + i * 2 + 1, 1)
                pairs(sp, (HP - 1) * B, HP * B, load)
                for s in range(2):
                    sp.wait_ge(stored[s], 32 * (STEPS // 2))

            @block.gpsimd
            def _(pool):
                nc.gpsimd.memset(V[:, :, :, :, HD:2 * HD], 1.0).then_inc(ones_set, 1)

                def values(n, s):
                    if not isinstance(n, int) or n >= 2:
                        hold(pool, summed, n - 1)
                    nc.gpsimd.tensor_copy(V[:, s, :, :, 0:HD],
                                          V_all[:, n, :].rearrange("p (t h d) -> p t h d", t=T, h=2)
                                          ).then_inc(v_ready, 1)

                def mask(n, s, h):
                    hold(pool, exped, n * NX + (NX - 1 + h))
                    blocks = prob[:, s, h, :].rearrange("p (t n) -> p t n", n=ROW)[:, :, 0:P]
                    nc.gpsimd.affine_select(blocks, blocks, pattern=[[0, T], [1, P]], compare_op=ALU.is_ge,
                                            fill=0.0, base=0, channel_multiplier=-1).then_inc(masked, 1)

                def step(n, s, ahead=True):
                    mask(n, s, 0)
                    mask(n, s, 1)
                    if ahead:
                        values(n + 1, 1 - s)

                values(0, 0)
                step(0, 0)
                pairs(pool, 1, STEPS - 1, step)
                step(STEPS - 1, (STEPS - 1) % 2, ahead=False)

            @block.vector
            def _(dve):
                def maximum(n, s, u, g):
                    hold(dve, scores, n * NU + (u + 1))
                    for i, (h, t, c) in enumerate(units[u]):
                        w = (t + 1) * P
                        last = nc.vector.tensor_tensor_reduce(
                            scaled[:, u, c:c + w], s_ps[u][:, c:c + w], table[:, g, h, N - w:N], 1.0, 0.0,
                            ALU.mult, ALU.max, top[:, u, i:i + 1])
                    last.then_inc(maxed, 1)

                def shift(n, s, u):
                    dve.wait_ge(maxed, n * NU + (u + 1))
                    if not isinstance(n, int) or n:
                        dve.wait_ge(turned, (n - 1) * NU + (u + 1))
                    for i, (h, t, c) in enumerate(units[u]):
                        w = (t + 1) * P
                        last = nc.vector.tensor_scalar(shifted[:, u, c:c + w], scaled[:, u, c:c + w], 0.0,
                                                       top[:, u, i:i + 1], ALU.max, ALU.subtract)
                    last.then_inc(relued, 1)

                def step(n, s, g, prev=True):
                    for u in range(NU):
                        maximum(n, s, u, g)
                        if u:
                            shift(n, s, u - 1)
                        elif prev:
                            shift(n - 1, 1 - s, NU - 1)

                def heads(hp, g, first=0):
                    with dve.Fori(first // 2, B // 2) as i:
                        for s in range(2):
                            step(hp * B + (i * 2 + s), s, g)

                dve.wait_ge(table_in[0], 16)
                step(0, 0, 0, prev=False)
                step(1, 1, 0)
                heads(0, 0, 2)
                dve.wait_ge(table_in[1], 16)
                heads(1, 1)
                with dve.Fori(1, HP // 2) as p:
                    for g in range(2):
                        hold(dve, table_in[g], (p + 1) * 16)
                        heads(p * 2 + g, g)
                shift(STEPS - 1, 1, NU - 1)

            @block.tensor
            def _(pe):
                def score(n, s, u):
                    if u == 0:
                        pe.wait_ge(q_in[s], (n // 2 + 1) * 48)
                        pe.wait_ge(k_in[s], (n // 2 + 1) * 48)
                    if not isinstance(n, int) or n:
                        pe.wait_ge(maxed, (n - 1) * NU + (u + 1))
                    for h, t, c in units[u]:
                        w = (t + 1) * P
                        last = nc.tensor.matmul(s_ps[u][:, c:c + w], Q[:, s, h * N + t * P:h * N + w],
                                                K[:, s, h * N:h * N + w], start=True, stop=True)
                    last.then_inc(scores, 1)

                def turn(n, s, u):
                    pe.wait_ge(relued, n * NU + (u + 1))
                    if not isinstance(n, int) or n * NU + u >= 2:
                        pe.wait_ge(exped, n * NX + sum(len(x) for x in units[:u - 1]) if u else
                                   (n - 1) * NX + sum(len(x) for x in units[:NU - 1]))
                    for c in range(0, N, P):
                        last = nc.tensor.transpose(bank(t_ps, s, u)[:, c:c + P], shifted[:, u, c:c + P], ident[:, :])
                    last.then_inc(turned, 1)

                def context_of(n, s, j):
                    if j == 0:
                        pe.wait_ge(v_ready, n + 1)
                        if not isinstance(n, int) or n:
                            pe.wait_ge(copied, n)
                        pe.wait_ge(masked, n * 2 + 2)
                    for h in range(2):
                        rows = prob[:, s, h, 0:T * N].rearrange("p (t n) -> p t n", n=N)[:, j:T, j * P:(j + 1) * P]
                        last = nc.tensor.matmul(
                            o_ps[2 * HD * h:2 * HD * (h + 1), j * P:N].rearrange("p (t n) -> p t n", n=P),
                            V[:, s, j, h, :], rows,
                            start=(j == 0), stop=(j == T - 1))
                    if j == T - 1:
                        last.then_inc(summed, 1)

                def step(n, s, prev=True, following=True):
                    for u in range(NU):
                        if u + LEAD < NU:
                            score(n, s, u + LEAD)
                        elif following:
                            score(n + 1, 1 - s, u + LEAD - NU)
                        turn(n, s, u)
                        if prev:
                            for j in WHEN[u]:
                                context_of(n - 1, 1 - s, j)

                pe.wait_ge(ones_set, 1)
                for u in range(LEAD):
                    score(0, 0, u)
                step(0, 0, prev=False)
                step(1, 1)
                pairs(pe, 2, STEPS - 1, step)
                step(STEPS - 1, 1, following=False)
                for j in range(T):
                    context_of(STEPS - 1, 1, j)

            @block.scalar
            def _(act):
                def copy(n, s):
                    act.wait_ge(summed, n + 1)
                    if not isinstance(n, int) or n >= 2:
                        act.wait_ge(stored[s], (n // 2) * 32)
                    nc.scalar.copy(ctxT[:, s, :], o_ps[:, :]).then_inc(copied, 1)

                def store(n, s):
                    act.wait_ge(copied, n + 1)
                    for h in range(2):
                        act.dma_start(dram["ctx"][n % B, n // B, h], ctxT[2 * HD * h:2 * HD * h + HD + 1, s, :]
                                      ).then_inc(stored[s], 16)

                def step(n, s, prev=True, before=True):
                    for u in range(NU):
                        act.wait_ge(turned, n * NU + (u + 1))
                        if u == 0 and (not isinstance(n, int) or n >= 2):
                            act.wait_ge(summed, n - 1)
                        for h, t, c in units[u]:
                            w = (t + 1) * P
                            nc.scalar.activation(prob[:, s, h, t * N:t * N + w], bank(t_ps, s, u)[:, c:c + w],
                                                 ACT.Exp).then_inc(exped, 1)
                        if u == 1 and before:
                            store(n - 2, s)
                    if prev:
                        copy(n - 1, 1 - s)

                step(0, 0, prev=False, before=False)
                step(1, 1, before=False)
                pairs(act, 2, STEPS, step)
                copy(STEPS - 1, 1)
                store(STEPS - 2, 0)
                store(STEPS - 1, 1)


def feed(nc, a, keep, dram, X_all, weights):
    up, down = weights
    with ExitStack() as ctx:
        kit = Kit(nc, ctx, "feed_")
        ident = keep["ident"]
        Wo = kit.sb("Wo", [P, KD, D])
        supT = kit.sb("supT", [P, KD, HID])
        sdownT = kit.sb("sdownT", [P, len(HT), D])
        gateT = kit.sb("gateT", [P, KD, E])
        bo = kit.sb("bo", [P, D])
        ebias = kit.sb("ebias", [P, E])
        den = kit.sb("den", [P, B, N // 8])
        half = kit.sb("half", [P, T])
        iota_e = kit.sb("iota_e", [P, E])
        before = kit.sb("before", [P, P], BF16)
        ones = kit.sb("ones", [P, P], BF16)
        x = kit.sb("x", [P, 2, T, D])
        ga = kit.sb("ga", [P, 2, D])
        num = kit.sb("num", [P, 2, KD, N])
        inv = kit.sb("inv", [P, 2, KD, N])
        mod2 = kit.sb("mod2", [P, 2, 2, D])
        gb = kit.sb("gb", [P, 2, D])
        CT = kit.sb("CT", [P, 2, KD, N])
        gabo = kit.sb("gabo", [P, 2, D])
        xb = kit.sb("xb", [P, 2, T, D])
        Wog = kit.sb("Wog", [P, 2, KD, D])
        stats = kit.sb("stats", [P, 2, T, 6])
        mv = kit.sb("mv", [P, 2, T, 2])
        var = kit.sb("var", [P, 2, T])
        rstd = kit.sb("rstd", [P, 2, T])
        xn = kit.sb("xn", [P, T, D])
        xm = kit.sb("xm", [P, T, D])
        h = kit.sb("h", [P, 2, T, D])
        hT = kit.sb("hT", [P, 2, KD, N])
        relu = kit.sb("relu", [P, len(HT), N])
        hid = kit.sb("hid", [P, len(HT), N])
        shared = kit.sb("shared", [P, T, D])
        e = kit.sb("e", [P, T, E])
        e1 = kit.sb("e1", [P, T, E])
        score = kit.sb("score", [P, T, E])
        biased = kit.sb("biased", [P, T, E])
        best = kit.sb("best", [P, T, 8])
        which = kit.sb("which", [P, T, 8], U32)
        whichf = kit.sb("whichf", [P, 2, T])
        hot = kit.sb("hot", [P, 2, T, E])
        picked = kit.sb("picked", [P, T, E], BF16)
        prod = kit.sb("prod", [P, 2, T, E])
        prod2 = kit.sb("prod2", [P, 2, T, E])
        weight = kit.sb("weight", [P, 2, 2, T])
        base = kit.sb("base", [P, 2, E])
        pos = kit.sb("pos", [P, T, E])
        posf = kit.sb("posf", [P, 2, T])
        place = kit.sb("place", [P, 2, 2, T], U32)
        ids = kit.sb("ids", [P, 2, 2, T])
        rows = kit.sb("rows", [P, 2, 2, T, ROWW], BF16)
        bank = [kit.ps(f"bank{i}", [P, 2, D]) for i in range(3)]
        ao, dn = [bank[1], bank[0]], [bank[2], bank[0]]
        tp = [kit.ps(f"tp{i}", [P, N]) for i in range(KD)]
        hp = [kit.ps(f"hp{i}", [P, N]) for i in range(2)]
        router_ps = kit.ps("router_ps", [P, 2 * T + 1, E])
        lg, rk = router_ps[:, 0:T, :], router_ps[:, T:, :]

        S = {n: kit.sem(n) for n in (
            "w_in", "w_in2", "den_in", "den_in2", "den_done", "inv_out", "set_up", "xb_done", "wog_done", "gabo_done", "ct", "ao_done", "x1",
            "stats", "mv", "var", "rstd", "xn", "xm", "h", "tp", "hT", "logits", "exp", "own", "mask", "rank",
            "place", "weight", "hidden", "relu", "hid", "down", "shared", "x1s", "rows", "ids", "held", "consts",
            "wgt_in", "wgt_zero", "pad_done")}
        ld0 = [kit.sem(f"ld0{s}") for s in range(2)]
        ld1 = [kit.sem(f"ld1{s}") for s in range(2)]
        ld2 = [kit.sem(f"ld2{s}") for s in range(2)]
        ld3 = [kit.sem(f"ld3{s}") for s in range(2)]
        sent = [kit.sem(f"sent{s}") for s in range(2)]
        M = len(HT)
        region = dram["region"]

        def later(b, k):
            return not isinstance(b, int) or b >= k

        def hold(eng, sem, value):
            eng.wait_ge(sem, value)
            eng.sem_inc(S["held"], 1)

        def steps(eng, step):
            step(0, 0, False, True, True)
            step(1, 1, True, True, True)
            pairs(eng, 2, B - 2, lambda b, s: step(b, s, True, True, True))
            step(B - 2, 0, True, True, False)
            step(B - 1, 1, True, False, False)

        with nc.Block() as block:

            @block.sync
            def _(sp):
                inv_rows = dram["inv"].rearrange("b (h n) -> b h n", n=N)

                def load_data(b, s):
                    sp.dma_start(x[:, s, :, :], a["x"][b].rearrange("(t p) d -> p t d", p=P)).then_inc(ld0[s], 16)
                    sp.dma_start(ga[:, s, :], dram["rows"][b, 0:1, :].partition_broadcast(P)).then_inc(ld0[s], 16)
                    for k in range(KD):
                        sp.dma_start(num[:, s, k, :], heads[b, k * 8:(k + 1) * 8, 0:HD, :]).then_inc(ld1[s], 16)

                def load_inv(b, s):
                    for k in range(KD):
                        sp.dma_start(inv[:, s, k, :], inv_rows[b, k * 8:(k + 1) * 8, :].unsqueeze(1).to_broadcast(
                            [8, HD, N])).then_inc(ld1[s], 16)

                def store_inv(first, last, count):
                    sp.wait_ge(S["den_done"], count)
                    sp.dma_start(dram["inv"].rearrange("b (p n) -> p b n", p=P)[:, first:last, :],
                                 den[:, first:last, :]).then_inc(S["inv_out"], 16)
                    sp.wait_ge(S["inv_out"], 16 * count)

                heads = dram["ctx"].rearrange("b g h r n -> b (g h) r n")

                def load_sums(b, sem):
                    sp.dma_start(den[:, b, :], heads[b, :, HD, :].rearrange("h (c n) -> h c n", c=8)).then_inc(sem, 16)

                def broadcast(dst, src, sem):
                    sp.dma_start(dst[:, :], a[src].unsqueeze(0).partition_broadcast(P)).then_inc(sem, 16)

                def weights(dst, src, sem):
                    sp.dma_start(dst[:, :, :], a[src].rearrange("(k p) n -> p k n", p=P)).then_inc(sem, 16)

                def load(b, s):
                    if later(b, 2):
                        sp.wait_ge(S["xb_done"], b - 1)
                        sp.wait_ge(S["wog_done"], b - 1)
                        sp.wait_ge(S["ct"], b - 1)
                    load_data(b, s)
                    load_inv(b, s)

                def load_mod(b, s):
                    if later(b, 2):
                        sp.wait_ge(S["h"], b - 1)
                    sp.dma_start(mod2[:, s, :, :], dram["rows"][b, 2:4, :].partition_broadcast(P)).then_inc(ld2[s], 16)

                def load_gate(b, s):
                    if later(b, 2):
                        sp.wait_ge(S["shared"], (b - 1) * 2)
                    sp.dma_start(gb[:, s, :], dram["rows"][b, 1:2, :].partition_broadcast(P)).then_inc(ld3[s], 16)

                def step(b, s):
                    load(b, s)
                    load_mod(b - 1, 1 - s)
                    load_gate(b - 2, s)

                for b in range(2):
                    load_sums(b, S["den_in"])
                weights(Wo, "Wo", S["w_in"])
                broadcast(bo, "bo", S["w_in"])
                load_data(0, 0)
                store_inv(0, 2, 1)
                load_inv(0, 0)
                load_mod(0, 0)
                weights(gateT, "gateT", S["w_in2"])
                broadcast(ebias, "bias", S["w_in2"])
                load_data(1, 1)
                load_inv(1, 1)
                weights(supT, "supT", S["w_in2"])
                for m, (c, size) in enumerate(HT):
                    sp.dma_start(sdownT[0:size, m, :], a["sdownT"][c:c + size]).then_inc(S["w_in2"], 16)
                for b in range(2, B):
                    load_sums(b, S["den_in2"])
                store_inv(2, B, 2)
                step(2, 0)
                step(3, 1)
                pairs(sp, 4, B, step)
                load_mod(B - 1, 1)
                load_gate(B - 2, 0)
                load_gate(B - 1, 1)

            @block.gpsimd
            def _(pool):
                nc.gpsimd.memset(half[:, :], -0.5).then_inc(S["set_up"], 1)
                nc.gpsimd.iota(iota_e[:, :], pattern=[[1, E]], base=0, channel_multiplier=0,
                               allow_small_or_imprecise_dtypes=True).then_inc(S["set_up"], 1)
                nc.gpsimd.iota(ids[:, 0, :, :], pattern=[[B * N, 2], [P, T]], base=0, channel_multiplier=1,
                               allow_small_or_imprecise_dtypes=True).then_inc(S["set_up"], 1)
                nc.gpsimd.iota(base[:, 0, :], pattern=[[CAP, E]], base=0, channel_multiplier=0,
                               allow_small_or_imprecise_dtypes=True).then_inc(S["set_up"], 1)
                nc.gpsimd.memset(ones[:, :], 1.0).then_inc(S["set_up"], 1)
                pool.wait_ge(S["set_up"], 5)
                nc.gpsimd.affine_select(before[:, :], ones[:, :], pattern=[[1, P]], compare_op=ALU.is_gt, fill=0.0,
                                        base=0, channel_multiplier=-1).then_inc(S["consts"], 1)
                pool.wait_ge(S["w_in"], 32)

                def prep(b, s):
                    pool.wait_ge(ld0[s], (b // 2 + 1) * 32)
                    if later(b, 2):
                        pool.wait_ge(S["xb_done"], b - 1)
                    nc.gpsimd.tensor_tensor(gabo[:, s, :], ga[:, s, :], bo[:, :], ALU.mult).then_inc(S["gabo_done"], 1)
                    if later(b, 2):
                        pool.wait_ge(S["x1"], (b - 1) * 2)
                    nc.gpsimd.tensor_tensor(Wog[:, s, :, :], Wo[:, :, :],
                                            ga[:, s, :].unsqueeze(1).to_broadcast([P, KD, D]), ALU.mult
                                            ).then_inc(S["wog_done"], 1)
                    pool.wait_ge(S["gabo_done"], b + 1)
                    nc.gpsimd.tensor_tensor(xb[:, s, :, :], x[:, s, :, :],
                                            gabo[:, s, :].unsqueeze(1).to_broadcast([P, T, D]), ALU.add
                                            ).then_inc(S["xb_done"], 1)

                def root(b, s):
                    pool.wait_ge(S["var"], b + 1)
                    nc.gpsimd.tensor_tensor(rstd[:, s, :], var[:, s, :], half[:, :], ALU.pow).then_inc(S["rstd"], 1)

                def send(b, s):
                    hold(pool, S["place"], b + 1)
                    hold(pool, S["ids"], b + 1)
                    for c in range(2):
                        for t in range(T):
                            hold(pool, S["rows"], b * (2 * T) + (c * T + t + 1))
                            pool.indirect_dma_start(
                                out=region, out_offset=bass.IndirectOffsetOnAxis(ap=place[:, s, c, t:t + 1], axis=0),
                                in_=rows[:, s, c, t, :], in_offset=None).then_inc(sent[s], 16)

                prep(0, 0)
                root(0, 0)
                prep(1, 1)
                nc.gpsimd.memset(up[:, :, :, HID:], 0.0).then_inc(S["wgt_zero"], 1)
                pool.wait_ge(S["wgt_zero"], 1)
                nc.gpsimd.memset(down[HID % P:, M - 1, :, :], 0.0).then_inc(S["wgt_zero"], 1)
                pool.wait_ge(S["wgt_zero"], 2)
                for k in range(KD):
                    pool.dma_start(up[:, k, :, 0:HID], a["upT"][k * P:(k + 1) * P]).then_inc(S["wgt_in"], 16)
                for m, (c, size) in enumerate(HT):
                    pool.dma_start(down[0:size, m, :, :], a["downT"][c:c + size]).then_inc(S["wgt_in"], 16)

                def step(b, s, prev, nxt, nxt2):
                    if nxt:
                        root(b + 1, 1 - s)
                    if nxt2:
                        prep(b + 2, s)
                    send(b, s)
                steps(pool, step)
                for s in range(2):
                    pool.wait_ge(sent[s], 16 * 2 * T * (B // 2))
                pool.wait_ge(S["wgt_in"], 16 * (KD + M))

            @block.vector
            def _(dve):
                dve.wait_ge(S["den_in"], 32)
                nc.vector.reciprocal(den[:, 0:2, :], den[:, 0:2, :]).then_inc(S["den_done"], 1)

                def normalise(b, s):
                    dve.wait_ge(ld1[s], (b // 2 + 1) * 64)
                    if later(b, 2):
                        dve.wait_ge(S["ao_done"], (b - 1) * 2)
                    nc.vector.tensor_tensor(CT[:, s, :, :], num[:, s, :, :], inv[:, s, :, :], ALU.mult
                                            ).then_inc(S["ct"], 1)

                def residual(b, s):
                    dve.wait_ge(S["xb_done"], b + 1)
                    for m in range(2):
                        dve.wait_ge(S["ao_done"], b * 2 + (m + 1))
                        nc.vector.tensor_tensor(X_all[:, bass.ds(b * T + 2 * m, 2), :], ao[m][:, :, :],
                                                xb[:, s, 2 * m:2 * m + 2, :], ALU.add).then_inc(S["x1"], 1)
                    hold(dve, S["x1"], b * 2 + 2)
                    for t in range(T):
                        nc.vector.bn_stats(stats[:, s, t, :], X_all[:, b * T + t, :]).then_inc(S["stats"], 1)
                    hold(dve, S["stats"], b * T + T)
                    for t in range(T):
                        nc.vector.bn_aggr(mv[:, s, t, :], stats[:, s, t, :]).then_inc(S["mv"], 1)
                    dve.wait_ge(S["mv"], b * T + T)
                    nc.vector.tensor_scalar(var[:, s, :], mv[:, s, :, 1], EPS, None, ALU.add).then_inc(S["var"], 1)

                def modulate(b, s):
                    dve.wait_ge(S["rstd"], b + 1)
                    if later(b, 1):
                        dve.wait_ge(S["xm"], b)
                    for t in range(T):
                        nc.vector.tensor_scalar(xn[:, t, :], X_all[:, b * T + t, :], mv[:, s, t, 0:1],
                                                rstd[:, s, t:t + 1], ALU.subtract, ALU.mult).then_inc(S["xn"], 1)
                    dve.wait_ge(ld2[s], (b // 2 + 1) * 16)
                    dve.wait_ge(S["xn"], b * T + T)
                    if later(b, 1):
                        dve.wait_ge(S["h"], b)
                    nc.vector.tensor_tensor(xm[:, :, :], xn[:, :, :], mod2[:, s, 0, :].unsqueeze(1).to_broadcast(
                        [P, T, D]), ALU.mult).then_inc(S["xm"], 1)
                    dve.wait_ge(S["xm"], b + 1)
                    if later(b, 2):
                        dve.wait_ge(S["rows"], (b - 1) * (2 * T))
                    nc.vector.tensor_tensor(h[:, s, :, :], xm[:, :, :], mod2[:, s, 1, :].unsqueeze(1).to_broadcast(
                        [P, T, D]), ALU.add).then_inc(S["h"], 1)

                def route(b, s):
                    n = b * CHAIN
                    if later(b, 1):
                        dve.wait_ge(S["own"], n)
                        dve.wait_ge(S["weight"], b)
                    dve.wait_ge(S["exp"], b + 1)
                    nc.vector.tensor_scalar(e1[:, :, :], e[:, :, :], 1.0, None, ALU.add).then_inc(S["own"], 1)
                    dve.wait_ge(S["own"], n + 1)
                    nc.vector.reciprocal(score[:, :, :], e1[:, :, :]).then_inc(S["own"], 1)
                    dve.wait_ge(S["own"], n + 2)
                    nc.vector.tensor_tensor(biased[:, :, :], score[:, :, :], ebias[:, :].unsqueeze(1).to_broadcast(
                        [P, T, E]), ALU.add).then_inc(S["own"], 1)
                    hold(dve, S["own"], n + 3)
                    for t in range(T):
                        nc.vector.max(best[:, t, :], biased[:, t, :]).then_inc(S["own"], 1)
                    hold(dve, S["own"], n + 3 + T)
                    for t in range(T):
                        nc.vector.max_index(which[:, t, :], best[:, t, :], biased[:, t, :]).then_inc(S["own"], 1)
                    dve.wait_ge(S["own"], n + 3 + 2 * T)
                    nc.vector.tensor_copy(whichf[:, :, :], which[:, :, 0:2].rearrange("p t c -> p c t")
                                          ).then_inc(S["own"], 1)
                    dve.wait_ge(S["own"], n + 4 + 2 * T)
                    for c in range(2):
                        nc.vector.tensor_tensor(hot[:, c, :, :], iota_e[:, :].unsqueeze(1).to_broadcast([P, T, E]),
                                                whichf[:, c, :].unsqueeze(2).to_broadcast([P, T, E]),
                                                ALU.is_equal).then_inc(S["own"], 1)
                    dve.wait_ge(S["own"], n + 6 + 2 * T)
                    if later(b, 1):
                        dve.wait_ge(S["rank"], b)
                    nc.vector.tensor_tensor(picked[:, :, :], hot[:, 0, :, :], hot[:, 1, :, :], ALU.add
                                            ).then_inc(S["mask"], 1)
                    nc.vector.tensor_tensor(prod[:, :, :, :], hot[:, :, :, :], score[:, :, :].unsqueeze(1).to_broadcast(
                        [P, 2, T, E]), ALU.mult).then_inc(S["own"], 1)
                    if later(b, 2):
                        dve.wait_ge(S["rows"], (b - 1) * (2 * T))
                    dve.wait_ge(S["own"], n + 7 + 2 * T)
                    nc.vector.tensor_reduce(weight[:, s, :, :], prod[:, :, :, :], AX.X, ALU.add
                                            ).then_inc(S["weight"], 1)

                def locate(b, s):
                    n = b * CHAIN + 7 + 2 * T
                    dve.wait_ge(S["rank"], b + 1)
                    nc.vector.tensor_tensor(pos[:, :, :], rk[:, 0:T, :], base[:, s, :].unsqueeze(1).to_broadcast(
                        [P, T, E]), ALU.add).then_inc(S["own"], 1)
                    nc.vector.tensor_tensor(base[:, 1 - s, :], rk[:, T, :], base[:, s, :], ALU.add
                                            ).then_inc(S["own"], 1)
                    dve.wait_ge(S["own"], n + 2)
                    nc.vector.tensor_tensor(prod2[:, :, :, :], hot[:, :, :, :], pos[:, :, :].unsqueeze(1).to_broadcast(
                        [P, 2, T, E]), ALU.mult).then_inc(S["own"], 1)
                    dve.wait_ge(S["own"], n + 3)
                    nc.vector.tensor_reduce(posf[:, :, :], prod2[:, :, :, :], AX.X, ALU.add).then_inc(S["own"], 1)
                    if later(b, 2):
                        dve.wait_ge(sent[s], (b // 2) * (16 * 2 * T))
                    dve.wait_ge(S["own"], n + 4)
                    nc.vector.tensor_copy(place[:, s, :, :], posf[:, :, :]).then_inc(S["place"], 1)
                    nc.vector.tensor_copy(rows[:, s, :, :, D:ROWW].bitcast(U32), ids[:, s, :, :].unsqueeze(3)
                                          ).then_inc(S["ids"], 1)
                    if later(b, 1):
                        dve.wait_ge(S["ids"], b)
                    nc.vector.tensor_scalar(ids[:, 1 - s, :, :], ids[:, s, :, :], float(N), None, ALU.add
                                            ).then_inc(S["own"], 1)

                def gate(b, s):
                    dve.wait_ge(ld3[s], (b // 2 + 1) * 16)
                    if later(b, 1):
                        dve.wait_ge(S["x1s"], b)
                    for m in range(2):
                        dve.wait_ge(S["down"], b * 2 + (m + 1))
                        nc.vector.tensor_tensor(shared[:, 2 * m:2 * m + 2, :], dn[m][:, :, :],
                                                gb[:, s, :].unsqueeze(1).to_broadcast([P, 2, D]), ALU.mult
                                                ).then_inc(S["shared"], 1)

                def finish(b, s):
                    dve.wait_ge(S["shared"], b * 2 + 2)
                    nc.vector.tensor_tensor(X_all[:, bass.ds(b * T, T), :], X_all[:, bass.ds(b * T, T), :],
                                            shared[:, :, :], ALU.add).then_inc(S["x1s"], 1)

                dve.wait_ge(S["set_up"], 5)
                normalise(0, 0)
                residual(0, 0)
                normalise(1, 1)
                modulate(0, 0)
                dve.wait_ge(S["den_in2"], 16 * (B - 2))
                nc.vector.reciprocal(den[:, 2:B, :], den[:, 2:B, :]).then_inc(S["den_done"], 1)
                dve.wait_ge(S["w_in2"], 96)

                def step(b, s, prev, nxt, nxt2):
                    if prev:
                        gate(b - 1, 1 - s)
                    if nxt:
                        residual(b + 1, 1 - s)
                    route(b, s)
                    if nxt:
                        modulate(b + 1, 1 - s)
                    if nxt2:
                        normalise(b + 2, s)
                    locate(b, s)
                    if prev:
                        finish(b - 1, 1 - s)
                steps(dve, step)
                gate(B - 1, 1)
                finish(B - 1, 1)
                dve.wait_ge(S["own"], B * CHAIN)
                nc.vector.tensor_copy(keep["ends"][:, :], base[:, 0, :]).then_inc(S["pad_done"], 1)

            @block.tensor
            def _(pe):
                def attention_out(b, s):
                    pe.wait_ge(S["ct"], b + 1)
                    pe.wait_ge(S["wog_done"], b + 1)
                    for m in range(2):
                        if m and later(b, 2):
                            pe.wait_ge(S["shared"], (b - 1) * 2)
                        for t2 in range(2):
                            t = 2 * m + t2
                            for k in range(KD):
                                last = nc.tensor.matmul(ao[m][:, t2, :], CT[:, s, k, t * P:(t + 1) * P],
                                                        Wog[:, s, k, :], start=(k == 0), stop=(k == KD - 1))
                        last.then_inc(S["ao_done"], 1)

                def turn(b, s):
                    pe.wait_ge(S["h"], b + 1)
                    for j in range(KD):
                        if later(b, 1):
                            pe.wait_ge(S["hT"], (b - 1) * KD + (j + 1))
                        for t in range(T):
                            last = nc.tensor.transpose(tp[j][:, t * P:(t + 1) * P], h[:, s, t, j * P:(j + 1) * P],
                                                       ident[:, :])
                        last.then_inc(S["tp"], 1)

                def router(b, s):
                    pe.wait_ge(S["hT"], b * KD + KD)
                    if later(b, 1):
                        pe.wait_ge(S["place"], b)
                    for t in range(T):
                        for k in range(KD):
                            last = nc.tensor.matmul(lg[:, t, :], hT[:, s, k, t * P:(t + 1) * P], gateT[:, k, :],
                                                    start=(k == 0), stop=(k == KD - 1))
                    last.then_inc(S["logits"], 1)

                def rank(b, s):
                    pe.wait_ge(S["mask"], b + 1)
                    pe.wait_ge(S["exp"], b + 1)
                    for t in range(T):
                        for j in range(t):
                            nc.tensor.matmul(rk[:, t, :], ones[:, :], picked[:, j, :], start=(j == 0), stop=False)
                        nc.tensor.matmul(rk[:, t, :], before[:, :], picked[:, t, :], start=(t == 0), stop=True)
                    for j in range(T):
                        last = nc.tensor.matmul(rk[:, T, :], ones[:, :], picked[:, j, :], start=(j == 0),
                                                stop=(j == T - 1))
                    last.then_inc(S["rank"], 1)

                def expand(b, s):
                    for m, (c, size) in enumerate(HT):
                        if later(b, 1) or m >= 2:
                            pe.wait_ge(S["relu"], b * M + (m - 1))
                        for k in range(KD):
                            last = nc.tensor.matmul(hp[(s + m) % 2][0:size, :], supT[:, k, c:c + size], hT[:, s, k, :],
                                                    start=(k == 0), stop=(k == KD - 1))
                        last.then_inc(S["hidden"], 1)

                def contract(b, s):
                    if not (isinstance(b, int) and b == B - 1):
                        pe.wait_ge(S["x1"], (b + 1) * 2 + 2)
                    for t, js in ((0, (0, 1)), (2, (0, 1)), (0, (2,)), (2, (2,)), (1, (0, 1, 2)), (3, (0, 1, 2))):
                        pe.wait_ge(S["hid"], b * M + (js[-1] + 1))
                        for j in js:
                            size = HT[j][1]
                            last = nc.tensor.matmul(dn[t // 2][:, t % 2, :], hid[0:size, j, t * P:(t + 1) * P],
                                                    sdownT[0:size, j, :], start=(j == 0), stop=(j == M - 1))
                        if t % 2:
                            last.then_inc(S["down"], 1)

                attention_out(0, 0)
                turn(0, 0)
                pe.wait_ge(S["w_in2"], 96)
                pe.wait_ge(S["consts"], 1)

                def step(b, s, prev, nxt, nxt2):
                    if nxt:
                        attention_out(b + 1, 1 - s)
                    router(b, s)
                    expand(b, s)
                    rank(b, s)
                    contract(b, s)
                    if nxt:
                        turn(b + 1, 1 - s)
                steps(pe, step)

            @block.scalar
            def _(act):
                def turned(b, s):
                    for j in range(KD):
                        act.wait_ge(S["tp"], b * KD + (j + 1))
                        nc.scalar.copy(hT[:, s, j, :], tp[j][:, :]).then_inc(S["hT"], 1)

                def squares(b, s):
                    for m, (c, size) in enumerate(HT):
                        act.wait_ge(S["hidden"], b * M + (m + 1))
                        nc.scalar.activation(relu[0:size, m, :], hp[(s + m) % 2][0:size, :], ACT.Relu
                                             ).then_inc(S["relu"], 1)
                        act.wait_ge(S["relu"], b * M + (m + 1))
                        if m == 0 and later(b, 1):
                            act.wait_ge(S["down"], b * 2)
                        nc.scalar.activation(hid[0:size, m, :], relu[0:size, m, :], ACT.Square).then_inc(S["hid"], 1)

                def scale(b, s):
                    act.wait_ge(S["weight"], b + 1)
                    if later(b, 2):
                        act.wait_ge(sent[s], (b // 2) * (16 * 2 * T))
                    for c in range(2):
                        for t in range(T):
                            nc.scalar.mul(rows[:, s, c, t, 0:D], h[:, s, t, :], weight[:, s, c, t:t + 1]
                                          ).then_inc(S["rows"], 1)

                turned(0, 0)

                def step(b, s, prev, nxt, nxt2):
                    act.wait_ge(S["logits"], b + 1)
                    if later(b, 1):
                        act.wait_ge(S["own"], (b - 1) * CHAIN + 1)
                    nc.scalar.activation(e[:, :, :], lg[:, :, :], ACT.Exp, scale=-1.0).then_inc(S["exp"], 1)
                    squares(b, s)
                    if nxt:
                        turned(b + 1, 1 - s)
                    scale(b, s)
                steps(act, step)


def experts(nc, a, keep, dram, weights):
    up, down = weights
    M = len(HT)
    with ExitStack() as ctx:
        kit = Kit(nc, ctx, "exp_")
        start = kit.sb("start", [P, E])
        tile_no = kit.sb("tile_no", [P, TILES])
        count = kit.sb("count", [P, E])
        counti = kit.sb("counti", [P, E], I32)
        tilesi = kit.sb("tilesi", [P, E], I32)
        tiles = kit.sb("tiles", [P, E])
        unit = kit.sb("unit", [P, E])
        upto = kit.sb("upto", [P, E])
        past = kit.sb("past", [P, TILES, E])
        pastn = kit.sb("pastn", [P, TILES, E])
        whose = kit.sb("whose", [P, TILES])
        first = kit.sb("first", [P, TILES])
        inside = kit.sb("inside", [P, TILES])
        inside2 = kit.sb("inside2", [P, TILES])
        rowf = kit.sb("rowf", [P, TILES])
        row_of = kit.sb("row_of", [P, TILES], U32)
        expert_of = kit.sb("expert_of", [P, TILES], U32)
        endi = kit.sb("endi", [P, E], U32)
        ident = kit.sb("identb", [P, P], BF16)
        rows = kit.sb("rows", [P, RING, T, ROWW], BF16)
        xT = kit.sb("xT", [P, RING, KD, BIG], BF16)
        relu = kit.sb("relu", [P, RING, M, BIG], BF16)
        hid = kit.sb("hid", [P, RING, M, BIG], BF16)
        ids = kit.sb("ids", [P, RING, T], U32)
        y = kit.sb("y", [P, RING, T, D], BF16)
        tp = [kit.ps(f"tp{i}", [P, KD, BIG], BF16) for i in range(2)]
        hp = [kit.ps(f"hp{m}", [P, BIG]) for m in range(M)]
        yp = [kit.ps(f"yp{i}", [P, 2, D]) for i in range(T // 2)]

        S = {n: kit.sem(n) for n in (
            "iotas", "own", "tables", "ends", "identb", "tp", "xT", "hidden", "relu", "hid", "yp",
            "y", "ids", "held")}
        rows_in = [kit.sem(f"rows_in{s}") for s in range(RING)]
        sent = [kit.sem(f"sent{s}") for s in range(RING)]

        def later(k, n):
            return not isinstance(k, int) or k >= n

        pads = [kit.sem(f"pads{i}") for i in range(2)]

        def pad_regions(eng, which, sem):
            eng.wait_ge(S["ends"], 1)
            for e in which:
                end = eng.value_load(endi[0:1, e:e + 1], min_val=e * CAP, max_val=(e + 1) * CAP - BIG)
                eng.dma_start(dram["region"][bass.ds(end, BIG), :],
                              dram["region"][E * CAP + (E + e) * BIG:E * CAP + (E + e + 1) * BIG, :]).then_inc(sem, 16)

        def hold(eng, sem, value):
            eng.wait_ge(sem, value)
            eng.sem_inc(S["held"], 1)

        def steps(eng, step):
            for k in range(RING):
                step(k, k, RING)
            with eng.Fori(1, TILES // RING - 1) as i:
                for r in range(RING):
                    step(i * RING + r, r, RING)
            for k in range((TILES // RING - 1) * RING, TILES):
                step(k, k % RING, min(RING, TILES - 1 - k))

        with nc.Block() as block:

            @block.sync
            def _(sp):
                pad_regions(sp, range(E // 2, E), pads[1])

            @block.gpsimd
            def _(pool):
                def iota(out, pattern, base, channel):
                    nc.gpsimd.iota(out, pattern=pattern, base=base, channel_multiplier=channel,
                                   allow_small_or_imprecise_dtypes=True).then_inc(S["iotas"], 1)

                iota(start[:, :], [[CAP, E]], 0, 0)
                iota(tile_no[:, :], [[1, TILES]], 0, 0)
                nc.gpsimd.memset(unit[:, :], 1.0).then_inc(S["iotas"], 1)

                def step(k, r, follow):
                    for t in range(T):
                        if t % 2 == 0:
                            hold(pool, S["y"], k * (T // 2) + (t // 2 + 1))
                        pool.indirect_dma_start(
                            out=dram["routed"], out_offset=bass.IndirectOffsetOnAxis(
                                ap=ids[:, r, t:t + 1], axis=0), in_=y[:, r, t, :], in_offset=None
                            ).then_inc(sent[r], 16)

                steps(pool, step)
                for r in range(RING):
                    pool.wait_ge(sent[r], 16 * T * len(range(r, TILES, RING)))

            @block.vector
            def _(dve):
                n = [0]

                def link(ins):
                    n[0] += 1
                    ins.then_inc(S["own"], 1)
                    dve.wait_ge(S["own"], n[0])

                v = nc.vector
                v.tensor_copy(ident[:, :], keep["ident"][:, :]).then_inc(S["identb"], 1)
                dve.wait_ge(S["iotas"], 3)
                v.tensor_copy(endi[:, :], keep["ends"][:, :]).then_inc(S["ends"], 1)
                link(v.tensor_tensor(count[:, :], keep["ends"][:, :], start[:, :], ALU.subtract))
                link(v.tensor_scalar(counti[:, :], count[:, :], float(BIG - 1), None, ALU.add))
                link(v.tensor_scalar(tilesi[:, :], counti[:, :], BIG.bit_length() - 1, None, ALU.arith_shift_right))
                link(v.tensor_copy(tiles[:, :], tilesi[:, :]))
                link(v.tensor_tensor_scan(upto[:, :], unit[:, :], tiles[:, :], 0.0, ALU.mult, ALU.add))
                link(v.tensor_tensor(past[:, :, :], tile_no[:, :].unsqueeze(2).to_broadcast([P, TILES, E]),
                                     upto[:, :].unsqueeze(1).to_broadcast([P, TILES, E]), ALU.is_ge))
                link(v.tensor_reduce(whose[:, :], past[:, :, :], AX.X, ALU.add))
                link(v.tensor_tensor(pastn[:, :, :], past[:, :, :],
                                     tiles[:, :].unsqueeze(1).to_broadcast([P, TILES, E]), ALU.mult))
                link(v.tensor_reduce(first[:, :], pastn[:, :, :], AX.X, ALU.add))
                link(v.tensor_tensor(inside[:, :], tile_no[:, :], first[:, :], ALU.subtract))
                link(v.tensor_scalar(inside2[:, :], inside[:, :], float(BIG), None, ALU.mult))
                link(v.scalar_tensor_tensor(out=rowf[:, :], in0=whose[:, :], scalar=float(CAP), in1=inside2[:, :],
                                            op0=ALU.mult, op1=ALU.add))
                v.tensor_copy(row_of[:, :], rowf[:, :]).then_inc(S["tables"], 1)
                v.tensor_scalar(expert_of[:, :], whose[:, :], float(E - 1), None, ALU.min).then_inc(S["tables"], 1)

                def turned(k, r):
                    dve.wait_ge(S["tp"], k + 1)
                    if later(k, RING):
                        dve.wait_ge(sent[r], (k // RING) * (16 * T))
                    v.tensor_copy(xT[:, r, :, :], tp[r % 2][:, :, :]).then_inc(S["xT"], 1)
                    v.tensor_copy(ids[:, r, :], rows[:, r, :, D:ROWW].bitcast(U32)).then_inc(S["ids"], 1)

                def square(k, r):
                    for m in range(M):
                        dve.wait_ge(S["relu"], k * M + (m + 1))
                        v.tensor_tensor(hid[:, r, m, :], relu[:, r, m, :], relu[:, r, m, :], ALU.mult
                                        ).then_inc(S["hid"], 1)

                def step(k, r, follow):
                    square(k, r)
                    if follow:
                        turned(k + 1, (r + 1) % RING)

                turned(0, 0)
                steps(dve, step)

            @block.tensor
            def _(pe):
                def turn(k, r):
                    pe.wait_ge(rows_in[r], (k // RING + 1) * 16)
                    if later(k, 2):
                        pe.wait_ge(S["xT"], k - 1)
                    for j in range(KD):
                        for t in range(T):
                            last = nc.tensor.transpose(tp[r % 2][:, j, t * P:(t + 1) * P],
                                                       rows[:, r, t, j * P:(j + 1) * P], ident[:, :])
                    last.then_inc(S["tp"], 1)

                def expand(k, r):
                    e = expert(k)
                    pe.wait_ge(S["xT"], k + 1)
                    for m in range(M):
                        if later(k, 1):
                            pe.wait_ge(S["relu"], (k - 1) * M + (m + 1))
                        for j in range(KD):
                            last = nc.tensor.matmul(hp[m][:, :], up[:, j, e, m * P:(m + 1) * P], xT[:, r, j, :],
                                                    start=(j == 0), stop=(j == KD - 1))
                        last.then_inc(S["hidden"], 1)

                def contract(k, r):
                    e = expert(k)
                    pe.wait_ge(S["hid"], k * M + M)
                    for i in range(T // 2):
                        if later(k, 1):
                            pe.wait_ge(S["y"], (k - 1) * (T // 2) + (i + 1))
                        for t2 in range(2):
                            t = 2 * i + t2
                            for m in range(M):
                                last = nc.tensor.matmul(yp[i][:, t2, :], hid[:, r, m, t * P:(t + 1) * P],
                                                        down[:, m, e, :], start=(m == 0), stop=(m == M - 1))
                        last.then_inc(S["yp"], 1)

                def expert(k):
                    return pe.value_load(expert_of[0:1, bass.ds(k, 1)], min_val=0, max_val=E - 1)

                pe.wait_ge(S["identb"], 1)
                pe.wait_ge(S["tables"], 2)
                turn(0, 0)

                def step(k, r, follow):
                    expand(k, r)
                    if follow:
                        turn(k + 1, (r + 1) % RING)
                    if later(k, 1):
                        contract(k - 1, (r - 1) % RING)
                steps(pe, step)
                contract(TILES - 1, (TILES - 1) % RING)

            @block.scalar
            def _(act):
                def load(k, r):
                    if later(k, RING):
                        act.wait_ge(S["tp"], k - RING + 1)
                        act.wait_ge(S["ids"], k - RING + 1)
                    row = act.value_load(row_of[0:1, bass.ds(k, 1)], min_val=0, max_val=E * CAP + (E - 1) * BIG)
                    act.dma_start(rows[:, r, :, :], dram["region"][bass.ds(row, BIG), :].rearrange(
                        "(t p) c -> p t c", p=P)).then_inc(rows_in[r], 16)

                def output(k, r):
                    for i in range(T // 2):
                        act.wait_ge(S["yp"], k * (T // 2) + (i + 1))
                        nc.scalar.copy(y[:, r, 2 * i:2 * i + 2, :], yp[i][:, :, :]).then_inc(S["y"], 1)

                def step(k, r, follow):
                    for m in range(M):
                        act.wait_ge(S["hidden"], k * M + (m + 1))
                        nc.scalar.activation(relu[:, r, m, :], hp[m][:, :], ACT.Relu).then_inc(S["relu"], 1)
                    if follow >= AHEAD:
                        load(k + AHEAD, (r + AHEAD) % RING)
                    if later(k, 1):
                        output(k - 1, (r - 1) % RING)

                pad_regions(act, range(E // 2), pads[0])
                act.wait_ge(S["tables"], 2)
                for p in pads:
                    act.wait_ge(p, 16 * (E // 2))
                for k in range(AHEAD):
                    load(k, k)
                steps(act, step)
                output(TILES - 1, (TILES - 1) % RING)


def merge(nc, keep, dram, X_all, out):
    with ExitStack() as ctx:
        kit = Kit(nc, ctx, "merge_")
        routed = kit.sb("routed", [P, RING, 2, T, D], BF16)
        gb = kit.sb("gb", [P, RING, D])
        both = kit.sb("both", [P, 2, T, D])
        gated = kit.sb("gated", [P, 2, T, D])
        o = kit.sb("o", [P, 2, T, D])
        r_in = [kit.sem(f"r_in{s}") for s in range(RING)]
        stored = [kit.sem(f"stored{s}") for s in range(2)]
        summed, gate, done = kit.sem("summed"), kit.sem("gate"), kit.sem("done")

        def later(b, k):
            return not isinstance(b, int) or b >= k

        with nc.Block() as block:

            @block.sync
            def _(sp):
                def load(b, r):
                    if later(b, RING):
                        sp.wait_ge(gate, b - RING + 1)
                    for c in range(2):
                        sp.dma_start(routed[:, r, c, :, :], dram["routed"][bass.ds(b * N + c * (B * N), N), :
                                                                           ].rearrange("(t p) d -> p t d", p=P)
                                     ).then_inc(r_in[r], 16)
                    sp.dma_start(gb[:, r, :], dram["rows"][b, 1:2, :].partition_broadcast(P)).then_inc(r_in[r], 16)
                for r in range(RING):
                    load(r, r)
                with sp.Fori(1, B // RING) as i:
                    for r in range(RING):
                        load(i * RING + r, r)

            @block.vector
            def _(dve):
                def step(b, r):
                    s = r % 2
                    dve.wait_ge(r_in[r], (b // RING + 1) * 48)
                    if later(b, 2):
                        dve.wait_ge(gate, b - 1)
                    nc.vector.tensor_tensor(both[:, s, :, :], routed[:, r, 0, :, :], routed[:, r, 1, :, :], ALU.add
                                            ).then_inc(summed, 1)
                    dve.wait_ge(summed, b + 1)
                    if later(b, 2):
                        dve.wait_ge(done, b - 1)
                    nc.vector.tensor_tensor(gated[:, s, :, :], both[:, s, :, :], gb[:, r, :].unsqueeze(1).to_broadcast(
                        [P, T, D]), ALU.mult).then_inc(gate, 1)
                for r in range(RING):
                    step(r, r)
                with dve.Fori(1, B // RING) as i:
                    for r in range(RING):
                        step(i * RING + r, r)

            @block.gpsimd
            def _(pool):
                def step(b, s):
                    pool.wait_ge(gate, b + 1)
                    if later(b, 2):
                        pool.wait_ge(stored[s], (b // 2) * 16)
                    nc.gpsimd.tensor_tensor(o[:, s, :, :], X_all[:, bass.ds(b * T, T), :], gated[:, s, :, :], ALU.add
                                            ).then_inc(done, 1)
                step(0, 0)
                step(1, 1)
                pairs(pool, 2, B, step)

            @block.scalar
            def _(act):
                def store(b, s):
                    act.wait_ge(done, b + 1)
                    act.dma_start(out[b].rearrange("(t p) d -> p t d", p=P), o[:, s, :, :]).then_inc(stored[s], 16)
                pairs(act, 0, B, store)
                for s in range(2):
                    act.wait_ge(stored[s], 16 * (B // 2))


def program(nc, a, out, stages=5):
    def scratch(name, shape, dt=F32):
        return nc.dram_tensor(name, shape, dt, kind="Internal").ap()

    dram = {
        "table": scratch("table_d", [HP, P, 2, N]),
        "rows": scratch("rows_d", [B, 4, D]),
        "q": scratch("q_d", [HP, B, PARTS, 32, N], BF16),
        "k": scratch("k_d", [HP, B, PARTS, 32, N], BF16),
        "ctx": scratch("ctx_d", [B, HP, 2, HD + 1, N]),
        "inv": scratch("inv_d", [B, H * N]),
        "region": scratch("region_d", [E * CAP + 2 * E * BIG, ROWW], BF16),
        "routed": scratch("routed_d", [2 * B * N + 2 * E * BIG, D], BF16),
    }
    with ExitStack() as ctx:
        kit = Kit(nc, ctx, "")
        keep = {"ident": kit.sb("ident", [P, P]), "modT": kit.sb("modT", [P, 2, KD, B]), "ends": kit.sb("ends", [P, E])}
        with ExitStack() as inner:
            V_all = Kit(nc, inner, "").sb("V_all", [P, STEPS, T * 2 * HD])
            for name, size in (("vrow", H), ("nw", H), ("top", H), ("dpos", N)):
                keep[name] = Kit(nc, inner, "").sb(name, [P, size])
            both = Kit(nc, inner, "")
            keep["pad"] = both.sb("pad", [P, 2 * E * T, ROWW], BF16)
            keep["padid"] = both.sb("padid", [P, 2 * E * T])
            keep["gate"], keep["mod2"] = both.sb("gate", [B, 2, D]), both.sb("mod2", [B, 2, D])
            keep["w"] = {n: both.sb(n, [P, KD, D]) for n in ("Wq", "Wk", "Wv")}
            keep["x"] = both.sb("x", [P, 2, T, D])
            keep["rows_out"], keep["w_in"] = both.sem("rows_out"), both.sem("w_in")
            keep["x_in"] = [both.sem(f"x_in{s}") for s in range(2)]
            prepare(nc, a, keep, dram)
            project(nc, a, keep, dram, V_all)
            if stages >= 3:
                attend(nc, a, keep, dram, V_all)
        if stages >= 4:
            X_all = kit.sb("X_all", [P, B * T, D])
            up = kit.sb("up", [P, KD, E, len(HT) * P], BF16)
            down = kit.sb("down", [P, len(HT), E, D], BF16)
            feed(nc, a, keep, dram, X_all, (up, down))
            if stages >= 5:
                experts(nc, a, keep, dram, (up, down))
                merge(nc, keep, dram, X_all, out)


def laid_out(i):
    import numpy as np
    def pair_order(w):
        return w.reshape(D, HP, 2, HD).transpose(0, 1, 3, 2).reshape(D, D)
    r = {
        "x": i["L0_attn_x"], "Wq": pair_order(i["L0_attn_Wq"]), "Wk": pair_order(i["L0_attn_Wk"]),
        "Wv": i["L0_attn_Wv"], "Wo": i["L0_attn_Wo"], "bo": i["L0_attn_bo"], "w": i["L0_attn_w"], "v": i["L0_attn_v"],
        "gateT": i["L0_ffn_gate_w"].T, "bias": i["L0_ffn_expert_bias"],
        "upT": i["L0_ffn_w_up"].transpose(2, 0, 1), "downT": i["L0_ffn_w_down"].transpose(2, 0, 1),
        "supT": i["L0_ffn_shared_w_up"].T, "sdownT": i["L0_ffn_shared_w_down"].T,
        "cT": i["L0_c"].T, "wmod": i["L0_wmod"],
    }
    return {k: np.ascontiguousarray(v) for k, v in r.items()}


def kernel(**inputs):
    import numpy as np
    import concourse.bacc as bacc
    from concourse.bass_utils import run_bass_kernel_spmd

    nc = bacc.Bacc("TRN2", target_bir_lowering=False, num_devices=1)
    arrays = laid_out({k: np.asarray(v) for k, v in inputs.items()})
    aps = {k: nc.dram_tensor("in_" + k, v.shape, mybir.dt.from_np(v.dtype), kind="ExternalInput").ap()
           for k, v in arrays.items()}
    out = nc.dram_tensor("out", (B, N, D), F32, kind="ExternalOutput").ap()
    program(nc, aps, out)
    r = run_bass_kernel_spmd(nc, [{"in_" + k: v for k, v in arrays.items()}], core_ids=[0])
    return r.results[0]["out"]
```
